# Optimizing a Trainium2 kernel written in Bass

```python
import numpy as np
import jax
import jax.numpy as jnp

def _softmax(x, axis=-1):
    return jax.nn.softmax(x, axis=axis)
def _gelu(x):
    return jax.nn.gelu(x, approximate=True)
def _silu(x):
    return jax.nn.silu(x)
def _sigmoid(x):
    return jax.nn.sigmoid(x)
def _layernorm(x, axis=-1, eps=1e-5):
    m = jnp.mean(x, axis=axis, keepdims=True)
    v = jnp.var(x, axis=axis, keepdims=True)
    return (x - m) / jnp.sqrt(v + eps)
def _scatter_add(tgt, idx, src, axis=0):
    return tgt.at[idx].add(src)
def _segment_sum(src, seg, n):
    return jax.ops.segment_sum(src, seg, n)

kernel_name = 'mk_conv_preact_d1_conv_nchw32_8ffce0'

def setup_inputs(seed: int = 0):
    np.random.seed(seed)
    _w = jnp.asarray
    def _rec_inputs():
        import jax
        import jax.numpy as jnp
        _gk = jax.random.key(seed)
        x = 7.572e-06 + 1 * jax.random.normal(jax.random.fold_in(_gk, 1), (4, 32, 384, 196), jnp.float32)
        return x
    x = _rec_inputs()
    def _L0_conv_setup():
        import jax, jax.numpy as jnp
        import numpy as np
        from jax import lax
        T, B, C, H, N = (4, 32, 384, 1536, 196)
        TAU = 1.5
        V_TH = 1.0
        EPS = 1e-05
        ALPHA = 2.0

        @jax.custom_vjp
        def spike_fn(v):
            return (v >= 0.0).astype(v.dtype)

        def _spike_fwd(v):
            return (spike_fn(v), v)

        def _spike_bwd(v, g):
            pi_half_alpha = np.pi / 2.0 * ALPHA
            grad = ALPHA / 2.0 / (1.0 + (pi_half_alpha * v) ** 2)
            return (g * grad,)
        spike_fn.defvjp(_spike_fwd, _spike_bwd)

        def lif(x_seq):

            def step(v, x):
                v = v + (x - v) / TAU
                s = spike_fn(v - V_TH)
                s_d = lax.stop_gradient(s)
                v = v * (1.0 - s_d)
                return (v, s)
            _, s_seq = lax.scan(step, jnp.zeros_like(x_seq[0]), x_seq)
            return s_seq

        def batchnorm(x, gamma, beta):
            mean = jnp.mean(x, axis=(0, 1, 3), keepdims=True)
            var = jnp.var(x, axis=(0, 1, 3), keepdims=True)
            g = gamma[None, None, :, None]
            b = beta[None, None, :, None]
            return g * (x - mean) * lax.rsqrt(var + EPS) + b
        key = jax.random.key(seed)
        ks = jax.random.split(key, 4)
        return {'x': jax.random.normal(ks[0], (T, B, C, N), jnp.float32), 'fc1_w': jax.random.normal(ks[1], (H, C), jnp.float32) / np.float32(np.sqrt(C)), 'fc1_b': jnp.zeros((H,), jnp.float32), 'fc1_gamma': jnp.ones((H,), jnp.float32), 'fc1_beta': jnp.zeros((H,), jnp.float32), 'fc2_w': jax.random.normal(ks[2], (C, H), jnp.float32) / np.float32(np.sqrt(H)), 'fc2_b': jnp.zeros((C,), jnp.float32), 'fc2_gamma': jnp.ones((C,), jnp.float32), 'fc2_beta': jnp.zeros((C,), jnp.float32)}
    _L0_conv_all = _L0_conv_setup()
    _L0_conv_in = {k: v for k, v in _L0_conv_all.items() if k in ('fc1_w', 'fc1_b', 'fc1_gamma', 'fc1_beta', 'fc2_w', 'fc2_b', 'fc2_gamma', 'fc2_beta', )}
    del _L0_conv_all

    return {
        "x": x,
        "L0_conv_fc1_w": _L0_conv_in["fc1_w"],
        "L0_conv_fc1_b": _L0_conv_in["fc1_b"],
        "L0_conv_fc1_gamma": _L0_conv_in["fc1_gamma"],
        "L0_conv_fc1_beta": _L0_conv_in["fc1_beta"],
        "L0_conv_fc2_w": _L0_conv_in["fc2_w"],
        "L0_conv_fc2_b": _L0_conv_in["fc2_b"],
        "L0_conv_fc2_gamma": _L0_conv_in["fc2_gamma"],
        "L0_conv_fc2_beta": _L0_conv_in["fc2_beta"],
    }

def reference(x, L0_conv_fc1_w, L0_conv_fc1_b, L0_conv_fc1_gamma, L0_conv_fc1_beta, L0_conv_fc2_w, L0_conv_fc2_b, L0_conv_fc2_gamma, L0_conv_fc2_beta):
    import jax
    import jax.numpy as jnp
    def _L0_conv_ref(x, fc1_w, fc1_b, fc1_gamma, fc1_beta, fc2_w, fc2_b, fc2_gamma, fc2_beta):
        import jax, jax.numpy as jnp
        import numpy as np
        from jax import lax
        T, B, C, H, N = (4, 32, 384, 1536, 196)
        TAU = 1.5
        V_TH = 1.0
        EPS = 1e-05
        ALPHA = 2.0

        @jax.custom_vjp
        def spike_fn(v):
            return (v >= 0.0).astype(v.dtype)

        def _spike_fwd(v):
            return (spike_fn(v), v)

        def _spike_bwd(v, g):
            pi_half_alpha = np.pi / 2.0 * ALPHA
            grad = ALPHA / 2.0 / (1.0 + (pi_half_alpha * v) ** 2)
            return (g * grad,)
        spike_fn.defvjp(_spike_fwd, _spike_bwd)

        def lif(x_seq):

            def step(v, x):
                v = v + (x - v) / TAU
                s = spike_fn(v - V_TH)
                s_d = lax.stop_gradient(s)
                v = v * (1.0 - s_d)
                return (v, s)
            _, s_seq = lax.scan(step, jnp.zeros_like(x_seq[0]), x_seq)
            return s_seq

        def batchnorm(x, gamma, beta):
            mean = jnp.mean(x, axis=(0, 1, 3), keepdims=True)
            var = jnp.var(x, axis=(0, 1, 3), keepdims=True)
            g = gamma[None, None, :, None]
            b = beta[None, None, :, None]
            return g * (x - mean) * lax.rsqrt(var + EPS) + b
        h = batchnorm(x, fc2_gamma, fc2_beta)
        h = lif(h)
        h = jnp.einsum('tbcn,hc->tbhn', h, fc1_w) + fc1_b[None, None, :, None]
        h = batchnorm(h, fc1_gamma, fc1_beta)
        h = lif(h)
        out = jnp.einsum('tbhn,ch->tbcn', h, fc2_w) + fc2_b[None, None, :, None]
        return out

    def _gn(v, G=16, eps=1e-5):
        B_, C_, H_, W_ = v.shape
        g = v.reshape(B_, G, C_ // G, H_, W_)
        m = jnp.mean(g, axis=(2, 3, 4), keepdims=True)
        s = jnp.var(g, axis=(2, 3, 4), keepdims=True)
        return ((g - m) / jnp.sqrt(s + eps)).reshape(v.shape)

    def _ln_c(v, eps=1e-6):
        m = jnp.mean(v, axis=1, keepdims=True)
        s = jnp.var(v, axis=1, keepdims=True)
        return (v - m) / jnp.sqrt(s + eps)

    def _ln_t(v, eps=1e-5):
        m = jnp.mean(v, axis=-1, keepdims=True)
        s = jnp.var(v, axis=-1, keepdims=True)
        return (v - m) / jnp.sqrt(s + eps)

    def _to_tokens(v):
        B_, C_, H_, W_ = v.shape
        return v.reshape(B_, C_, H_ * W_).transpose(0, 2, 1)
    def _from_tokens(t, like):
        B_, C_, H_, W_ = like.shape
        return t.transpose(0, 2, 1).reshape(B_, C_, H_, W_)

    x = x + _L0_conv_ref(_gn(x), L0_conv_fc1_w, L0_conv_fc1_b, L0_conv_fc1_gamma, L0_conv_fc1_beta, L0_conv_fc2_w, L0_conv_fc2_b, L0_conv_fc2_gamma, L0_conv_fc2_beta)
    return x


_drawn_inputs = setup_inputs


def setup_inputs(seed=0):
    import zlib

    import numpy as np

    out = dict(_drawn_inputs(seed))
    spreads = {'L0_conv_fc1_b': (0.0, 0.1),
     'L0_conv_fc1_gamma': (1.0, 0.2),
     'L0_conv_fc1_beta': (0.0, 0.1),
     'L0_conv_fc2_b': (0.0, 0.1),
     'L0_conv_fc2_gamma': (1.0, 0.2),
     'L0_conv_fc2_beta': (0.0, 0.1)}
    factors = {}
    for name, (base, spread) in spreads.items():
        noise = np.random.default_rng([zlib.crc32(name.encode()), seed]).standard_normal(out[name].shape)
        drawn = base * np.exp(spread * noise) if base else spread * noise
        out[name] = jnp.asarray(drawn.astype(out[name].dtype))
    for name, factor in factors.items():
        out[name] = (out[name] * factor).astype(out[name].dtype)
    return out
```

```python
from contextlib import ExitStack

import concourse.bass as bass
from concourse import mybir

F32 = mybir.dt.float32
F16 = mybir.dt.float16
F8 = mybir.dt.float8e4
I32 = mybir.dt.int32
U32 = mybir.dt.uint32
ALU = mybir.AluOpType
ACT = mybir.ActivationFunctionType
AX = mybir.AxisListType

T, B, C, H, N = 4, 32, 384, 1536, 196
P = 128
PAIR = 2
G = B // PAIR
PN = PAIR * N
TN = T * PN
KC = C // P
HC = H // P
TOKENS = T * B * N
TAU = 1.5
EPS = 1e-5

XRING = 4
TOK = 112
NQ = TN // TOK // 2
STRING = 4
HP = HC // 2
G1_JOBS = HC
G2_JOBS = KC
COVSCALE = 16384.0


def spiking_mlp(nc, x, fc1_w, fc1_b, fc1_gamma, fc1_beta, fc2_w, fc2_b, fc2_gamma, fc2_beta, out):
    with ExitStack() as ctx:
        def sb(name, shape, dt):
            return ctx.enter_context(nc.sbuf_tensor(name, shape, dt))

        def sem(name):
            return ctx.enter_context(nc.semaphore(name))

        ctx.enter_context(nc.allow_non_contiguous_dma(reason="per-channel parameters, a few KB"))

        w1_hi = sb("w1_hi", [P, KC, H], F16)
        w1_lo = sb("w1_lo", [P, KC, H], F16)
        w2_hi = sb("w2_hi", [P, HC, C], F16)
        w2_lo = sb("w2_lo", [P, HC, C], F16)
        spikes1 = sb("spikes1", [P, 2, KC, TN], F8)
        ident = sb("ident", [P, P], F32)
        ident8 = sb("ident8", [P, P], F8)
        ones = sb("ones", [P, P], F32)
        affine1 = sb("affine1", [P, G, 2 * T * KC], F32)
        affine1_now = sb("affine1_now", [P, XRING, 2 * T * KC], F32)
        par1 = sb("par1", [P, 3, HC], F32)
        par2 = sb("par2", [P, 3, KC], F32)
        scale1 = sb("scale1", [P, 2, HC], F32)
        scale2 = sb("scale2", [P, 2, KC], F32)
        affine2 = sb("affine2", [P, 2, HC], F32)
        tiny = sb("tiny", [P, 12, HC], F32)

        spikes1_all = sb("spikes1_all", [P, G * KC * TN // 4], U32)
        early = spikes1_all[:, :].bitcast(F32)
        at = [0]

        def early_view(cols):
            at[0] += cols
            return early[:, at[0] - cols:at[0]]

        w1_nat = early_view(HC * C).rearrange("p (m c) -> p m c", m=HC)
        w2_nat = early_view(KC * H).rearrange("p (k h) -> p k h", k=KC)
        w_turned = early_view(4 * 512).rearrange("p (r n) -> p r n", r=4)
        NS = G * T * KC
        stats = early_view(NS * 6)
        mu, m2, tmp_a, tmp_b = (early_view(NS) for _ in range(4))
        gn_mean, gn_var, gn_rstd, gn_tmp, gn_shift = (early_view(G * T) for _ in range(5))

        XT = T * KC * PN
        QW = 2 * C
        ARENA = XRING * XT + KC * PN + STRING * QW // 2
        arena = sb("arena", [P, ARENA], F32)
        x_ring = arena[:, 0:XRING * XT].rearrange("p (r t k n) -> p r t k n", r=XRING, t=T, k=KC)
        lif1_state = arena[:, XRING * XT:XRING * XT + KC * PN]
        spikes_turned = arena[:, XRING * XT + KC * PN:ARENA].bitcast(F16).rearrange(
            "p (r i c) -> p r i c", r=STRING, i=2)
        w1_again = arena[:, 0:HC * C].rearrange("p (m c) -> p m c", m=HC)
        CW = C + 1
        o = XT
        cov = arena[:, o:o + KC * CW].rearrange("p (k c) -> p k c", k=KC)
        o += KC * CW + 1
        cov_hi = arena[:, o:o + KC * 193].bitcast(F16).rearrange("p (k c) -> p k c", k=KC)[:, :, 0:CW]
        o += KC * 193
        cov_lo = arena[:, o:o + KC * 193].bitcast(F16).rearrange("p (k c) -> p k c", k=KC)[:, :, 0:CW]
        o += KC * 193
        diag = arena[:, o:o + C].rearrange("p (k c) -> p k c", k=KC)
        o += C
        rate_row = arena[:, o:o + C]
        o += C
        outer = arena[:, o:o + C]
        assert o + C <= 2 * XT
        prod = arena[:, 2 * XT:2 * XT + 2 * C].rearrange("p (r c) -> p r c", r=2)
        hid = arena[:, 0:4 * TN].rearrange("p (r m n) -> p r m n", r=2, m=2)
        o = 4 * TN
        spikes2 = arena[:, o:o + 2 * HC * TN // 4].bitcast(F8).rearrange("p (r m n) -> p r m n", r=2, m=HC)
        o += 2 * HC * TN // 4
        resid = arena[:, o:o + KC * TN].rearrange("p (k n) -> p k n", k=KC)
        o += KC * TN
        lif2_state = arena[:, o:o + 2 * PN].rearrange("p (m n) -> p m n", m=2)
        assert o + 2 * PN <= ARENA

        psum = ctx.enter_context(nc.psum_tensor("psum", [P, 8, 512], F32))
        gram = [psum[:, 0, 0:C], psum[:, 1, 0:C - P], psum[:, 2, 0:C - 2 * P]]
        GN_BANK, BLOCK_BANK, RATE_BANK = 7, 3, 4

        w_loaded = [sem("w1_loaded"), sem("w2_loaded")]
        par_loaded = sem("par_loaded")
        consts_set = sem("consts_set")
        w_scales = sem("w_scales")
        w_scaled = sem("w_scaled")
        w_transposed = sem("w_transposed")
        w_hi_set = sem("w_hi_set")
        w_lo_set = sem("w_lo_set")
        x_loaded = [sem(f"x_loaded{r}") for r in range(XRING)]
        x_free = sem("x_free")
        dve_step = sem("dve_step")
        gn_sums = sem("gn_sums")
        root_in = sem("root_in")
        root_out = sem("root_out")
        affine1_ready = sem("affine1_ready")
        affine1_copied = sem("affine1_copied")
        affine1_free = sem("affine1_free")
        y_act = sem("y_act")
        y_pool = sem("y_pool")
        lif1_step = sem("lif1_step")
        spikes1_ready = sem("spikes1_ready")
        spikes1_kept = [sem(f"spikes1_kept{r}") for r in range(2)]
        spikes1_turned = sem("spikes1_turned")
        turned = sem("turned")
        turned_free = sem("turned_free")
        turned_ready = sem("turned_ready")
        gram_step = sem("gram_step")
        zeros_set = sem("zeros_set")
        gram_copied = sem("gram_copied")
        blocks_turned = sem("blocks_turned")
        blocks_copied = sem("blocks_copied")
        diag_ready = sem("diag_ready")
        rates_ready = sem("rates_ready")
        cov_ready = sem("cov_ready")
        wcov_ready = sem("wcov_ready")
        wcov_read = sem("wcov_read")
        affine2_ready = sem("affine2_ready")
        spikes1_back = sem("spikes1_back")
        g1_done = sem("g1_done")
        g1_read = sem("g1_read")
        lif2_step = sem("lif2_step")
        spikes2_ready = sem("spikes2_ready")
        spikes2_free = sem("spikes2_free")
        results_out = sem("results_out")
        g2_done = sem("g2_done")
        g2_read = sem("g2_read")
        resid_loaded = [sem(f"resid_loaded{k}") for k in range(KC)]
        resid_biased = sem("resid_biased")
        stored = [sem(f"stored{k}") for k in range(KC)]
        waited = {e: sem(f"waited_{e}") for e in ("sp", "act", "dve", "pool", "pe")}

        def wait_first(eng, name, semaphore, value):
            eng.wait_ge(semaphore, value)
            if not isinstance(value, int):
                eng.sem_inc(waited[name], 1)

        def x_dram(t, g):
            return x[t, bass.ds(g * PAIR, PAIR), :, :]

        block = ctx.enter_context(nc.Block())

        @block.sync
        def _(sp):
            def load_tile(g, r):
                for t in range(T):
                    for k in range(KC):
                        sp.dma_start(x_ring[:, r, t, k, :].rearrange("p (b n) -> p b n", b=PAIR),
                                     x_dram(t, g)[:, k * P:(k + 1) * P, :].rearrange("b p n -> p b n")
                                     ).then_inc(x_loaded[r], 16)

            with sp.Fori(0, G // XRING) as i:
                for r in range(XRING):
                    wait_first(sp, "sp", x_free, i * XRING + (r + 1))
                    load_tile(i * XRING + r, r)
            for r in range(XRING):
                sp.wait_ge(x_free, G + r + 1)
                load_tile(r, r)

            def keep_spikes(g, r):
                wait_first(sp, "sp", spikes1_ready, g + 1)
                sp.dma_start(spikes1_all[:, bass.ds(g * (KC * TN // 4), KC * TN // 4)],
                             spikes1[:, r % 2, :, :].rearrange("p k n -> p (k n)").bitcast(U32)
                             ).then_inc(spikes1_kept[r % 2], 16)

            with sp.Fori(0, G // XRING - 1) as i:
                for r in range(XRING):
                    wait_first(sp, "sp", x_free, i * XRING + (G + XRING + r + 1))
                    load_tile(i * XRING + (XRING + r), r)
                    keep_spikes(i * XRING + r, r)
            sp.wait_ge(x_free, 2 * G + 1)
            sp.dma_start(w1_again, fc1_w.rearrange("(m p) c -> p m c", p=P)).then_inc(w_loaded[0], 16)
            for r in range(XRING):
                keep_spikes(G - XRING + r, r)

            def load_resid(n, k):
                for t in range(T):
                    sp.dma_start(resid[:, k, t * PN:(t + 1) * PN].rearrange("p (b n) -> p b n", b=PAIR),
                                 x_dram(t, n)[:, k * P:(k + 1) * P, :].rearrange("b p n -> p b n")
                                 ).then_inc(resid_loaded[k], 16)

            def store(n, k):
                wait_first(sp, "sp", g2_read, n * G2_JOBS + (k + 1))
                for t in range(T):
                    sp.dma_start(out[t, bass.ds(n * PAIR, PAIR), k * P:(k + 1) * P, :].rearrange("b p n -> p b n"),
                                 resid[:, k, t * PN:(t + 1) * PN].rearrange("p (b n) -> p b n", b=PAIR)
                                 ).then_inc(stored[k], 16)
                wait_first(sp, "sp", stored[k], n * (16 * T) + 16 * T)

            sp.wait_ge(affine2_ready, 1)
            for k in range(KC):
                load_resid(0, k)
            with sp.Fori(0, G - 1) as n:
                for k in range(KC):
                    store(n, k)
                    load_resid(n + 1, k)
            for k in range(KC):
                store(G - 1, k)

        @block.scalar
        def _(act):
            act.dma_start(w1_nat, fc1_w.rearrange("(m p) c -> p m c", p=P)).then_inc(w_loaded[0], 16)
            act.dma_start(w2_nat, fc2_w.rearrange("(k p) h -> p k h", p=P)).then_inc(w_loaded[1], 16)
            for i, v in enumerate((fc2_b, fc2_gamma, fc2_beta)):
                act.dma_start(par2[:, i, :], v.rearrange("(k p) -> p k", p=P)).then_inc(par_loaded, 16)
            for i, v in enumerate((fc1_b, fc1_gamma, fc1_beta)):
                act.dma_start(par1[:, i, :], v.rearrange("(m p) -> p m", p=P)).then_inc(par_loaded, 16)
            act.wait_ge(w_scales, 1)
            for m in range(HC):
                act.activation(w1_nat[:, m, :], w1_nat[:, m, :], ACT.Copy, scale=scale1[:, 0, m:m + 1]
                               ).then_inc(w_scaled, 1)
            act.wait_ge(w_scales, 2)
            for k in range(KC):
                act.activation(w2_nat[:, k, :], w2_nat[:, k, :], ACT.Copy, scale=scale2[:, 0, k:k + 1]
                               ).then_inc(w_scaled, 1)
            for q in range(9 + HC):
                act.wait_ge(w_transposed, q + 1)
                if q >= 4:
                    act.wait_ge(w_lo_set, q - 3)
                if q < 9:
                    cols, high = 512, w1_hi[:, q // 3, (q % 3) * 512:(q % 3 + 1) * 512]
                else:
                    cols, high = C, w2_hi[:, q - 9, :]
                act.activation(w_turned[:, q % 4, 0:cols], psum[:, q % 4, 0:cols], ACT.Copy).then_inc(w_hi_set, 1)
                act.activation(high, psum[:, q % 4, 0:cols], ACT.Copy).then_inc(w_hi_set, 1)
            for n in range(2):
                act.wait_ge(root_in, n + 1)
                src, dst = ((gn_var, gn_rstd), (tiny[:, 2, 0:KC], tiny[:, 3, 0:KC]))[n]
                act.activation(dst, src, ACT.Sqrt).then_inc(root_out, 1)

            act.sem_inc(affine1_free, XRING)
            act.sem_inc(turned_free, 2)

            def normalise(g, r, rounds):
                wait_first(act, "act", affine1_copied, g + 1)
                wait_first(act, "act", x_loaded[r], rounds)
                for t in range(T):
                    ins = act.activation(x_ring[:, r, t, 0, :], x_ring[:, r, t, 0, :], ACT.Identity,
                                         scale=affine1_now[:, r, t * KC:t * KC + 1],
                                         bias=affine1_now[:, r, T * KC + t * KC:T * KC + t * KC + 1])
                    ins.then_inc(y_act, 1)
                wait_first(act, "act", y_act, (g + 1) * T)
                act.sem_inc(affine1_free, 1)

            def turn_out(g, r):
                for q in range(NQ):
                    place = (r * NQ + q)
                    wait_first(act, "act", turned, g * NQ + (q + 1))
                    wait_first(act, "act", gram_step, g * NQ + (q + 1))
                    s = 4 + 2 * (place % 2)
                    act.activation(spikes_turned[0:TOK, place % STRING, :, :], psum[0:TOK, s:s + 2, 0:C], ACT.Copy
                                   ).then_inc(turned_ready, 1)
                    wait_first(act, "act", turned_ready, g * NQ + (q + 1))
                    act.sem_inc(turned_free, 1)

            X_ROUND = 16 * T * KC
            first = (G // XRING) * X_ROUND
            normalise(0, 0, first + X_ROUND)
            with act.Fori(0, G // XRING - 1) as i:
                for r in range(XRING):
                    normalise(i * XRING + (r + 1), (r + 1) % XRING,
                              i * X_ROUND + (first + (2 if r == XRING - 1 else 1) * X_ROUND))
                    turn_out(i * XRING + r, r)
            for r in range(XRING):
                if r < XRING - 1:
                    normalise(G - XRING + r + 1, r + 1, 2 * first)
                turn_out(G - XRING + r, r)

            act.wait_ge(gram_step, G * NQ + STRING)
            for k in range(KC):
                act.activation(cov[:, k, k * P:C], gram[k], ACT.Copy).then_inc(gram_copied, 1)
            act.wait_ge(blocks_turned, 1)
            act.activation(cov[:, 1, 0:P], psum[:, BLOCK_BANK, 0:P], ACT.Copy).then_inc(blocks_copied, 1)
            act.activation(cov[:, 2, 0:2 * P], psum[:, BLOCK_BANK, P:3 * P], ACT.Copy).then_inc(blocks_copied, 1)
            act.wait_ge(root_in, 3)
            act.activation(tiny[:, 3, :], tiny[:, 2, :], ACT.Sqrt).then_inc(root_out, 1)

            def hidden(s, m):
                wait_first(act, "act", g1_done, s * G1_JOBS + (m + 1))
                if isinstance(s, int) and s * HP + m // 2 < 2:
                    pass
                else:
                    wait_first(act, "act", spikes2_ready, s * HP + (m // 2 - 1))
                bank = 4 * job_set(s, m)
                act.activation(hid[:, (m // 2) % 2, m % 2, :].rearrange("p (t n) -> p t n", t=T),
                               psum[:, bank:bank + 4, 0:PN], ACT.Identity,
                               scale=affine2[:, 0, m:m + 1], bias=affine2[:, 1, m:m + 1]).then_inc(g1_read, 1)

            def job_set(s, m):
                if isinstance(s, int) and s == 0:
                    return m % 2
                return (m + m // 4 + parity[0]) % 2

            parity = [0]
            act.wait_ge(affine2_ready, 1)
            for m in range(HC):
                hidden(0, m)
            with act.Fori(0, (G - 2) // 2) as i:
                for u in range(2):
                    parity[0] = u
                    for m in range(HC):
                        hidden(i * 2 + (u + 1), m)
            parity[0] = 0
            for m in range(HC):
                hidden(G - 1, m)

        @block.vector
        def _(dve):
            count = [0]

            def link(ins):
                count[0] += 1
                ins.then_inc(dve_step, 1)
                dve.wait_ge(dve_step, count[0])

            dve.sem_inc(x_free, XRING)
            for n, (w, sc, rows) in enumerate(((w1_nat, scale1, HC), (w2_nat, scale2, KC))):
                dve.wait_ge(w_loaded[n], 16)
                big = tiny[:, 0, 0:rows]
                least = tiny[:, 1, 0:rows]
                link(dve.tensor_reduce(big, w, AX.X, ALU.max))
                link(dve.tensor_reduce(least, w, AX.X, ALU.min))
                link(dve.scalar_tensor_tensor(out=big, in0=least, scalar=-1.0, in1=big, op0=ALU.mult, op1=ALU.max))
                link(dve.tensor_scalar(big, big, 2.0 ** -100, None, ALU.max))
                expo = tiny[:, 1, 0:rows].bitcast(I32)
                link(dve.tensor_scalar(expo, big.bitcast(I32), 0x7F800000, None, ALU.bitwise_and))
                link(dve.tensor_scalar(sc[:, 0, :].bitcast(I32), expo, -1.0, float(268 << 23), ALU.mult, ALU.add))
                link(dve.tensor_scalar(sc[:, 1, :].bitcast(I32), expo, float(-(14 << 23)), None, ALU.add))
                dve.sem_inc(w_scales, 1)

            with dve.Fori(0, G // XRING) as i:
                for r in range(XRING):
                    wait_first(dve, "dve", x_loaded[r], i * (16 * T * KC) + 16 * T * KC)
                    for e in range(T * KC):
                        ins = dve.bn_stats(stats[:, bass.ds((i * XRING + r) * (6 * T * KC) + 6 * e, 6)],
                                           x_ring[:, r, e // KC, e % KC, :])
                    ins.then_inc(x_free, 1)
            dve.wait_ge(x_free, G + XRING)

            st = stats.rearrange("p (s v) -> p v s", v=6)
            link(dve.tensor_tensor(mu, st[:, 1, :], st[:, 4, :], ALU.add))
            link(dve.tensor_scalar(mu, mu, 0.5, None, ALU.mult))
            link(dve.tensor_tensor(tmp_a, st[:, 1, :], st[:, 4, :], ALU.subtract))
            link(dve.tensor_tensor(tmp_a, tmp_a, tmp_a, ALU.mult))
            link(dve.tensor_tensor(m2, st[:, 2, :], st[:, 5, :], ALU.add))
            link(dve.scalar_tensor_tensor(out=m2, in0=tmp_a, scalar=PN / 4.0, in1=m2, op0=ALU.mult, op1=ALU.add))
            link(dve.tensor_scalar(m2, m2, 1.0 / PN, None, ALU.mult))

            def by_chunk(v, k):
                return v.rearrange("p (s k) -> p k s", k=KC)[:, k, :]

            def newton_rsqrt(dst, var, tmp, n):
                dve.sem_inc(root_in, 1)
                dve.wait_ge(root_out, n)
                link(dve.reciprocal(dst, dst))
                link(dve.tensor_tensor(tmp, dst, dst, ALU.mult))
                link(dve.tensor_tensor(tmp, tmp, var, ALU.mult))
                link(dve.tensor_scalar(tmp, tmp, -0.5, 1.5, ALU.mult, ALU.add))
                link(dve.tensor_tensor(dst, dst, tmp, ALU.mult))

            dve.sem_inc(gn_sums, 1)
            sums = psum[:, GN_BANK, 0:G * T]
            dve.wait_ge(gn_sums, 2)
            link(dve.tensor_scalar(gn_mean, sums, 1.0 / C, None, ALU.mult))
            for k in range(KC):
                link(dve.tensor_tensor(by_chunk(mu, k), by_chunk(mu, k), gn_mean, ALU.subtract))
            link(dve.tensor_tensor(tmp_a, mu, mu, ALU.mult))
            link(dve.tensor_tensor(tmp_a, tmp_a, m2, ALU.add))
            dve.sem_inc(gn_sums, 1)
            dve.wait_ge(gn_sums, 4)
            link(dve.tensor_scalar(gn_var, sums, 1.0 / C, EPS, ALU.mult, ALU.add))
            newton_rsqrt(gn_rstd, gn_var, gn_tmp, 1)
            for k in range(KC):
                link(dve.tensor_tensor(by_chunk(mu, k), by_chunk(mu, k), gn_rstd, ALU.mult))
            bn_mean, bn_var, bn_rstd, bn_tmp, bn_scale = (tiny[:, i, 0:KC] for i in (1, 2, 3, 4, 5))
            link(dve.tensor_reduce(bn_mean, mu.rearrange("p (s k) -> p k s", k=KC), AX.X, ALU.add))
            link(dve.tensor_scalar(bn_mean, bn_mean, 1.0 / (G * T), None, ALU.mult))
            link(dve.tensor_tensor(gn_tmp, gn_rstd, gn_rstd, ALU.mult))
            for k in range(KC):
                link(dve.tensor_scalar(by_chunk(tmp_a, k), by_chunk(mu, k), bn_mean[:, k:k + 1], None, ALU.subtract))
                link(dve.tensor_tensor(by_chunk(tmp_b, k), by_chunk(m2, k), gn_tmp, ALU.mult))
            link(dve.tensor_tensor(tmp_a, tmp_a, tmp_a, ALU.mult))
            link(dve.tensor_tensor(tmp_a, tmp_a, tmp_b, ALU.add))
            link(dve.tensor_reduce(bn_var, tmp_a.rearrange("p (s k) -> p k s", k=KC), AX.X, ALU.add))
            link(dve.tensor_scalar(bn_var, bn_var, 1.0 / (G * T), EPS, ALU.mult, ALU.add))
            newton_rsqrt(bn_rstd, bn_var, bn_tmp, 2)
            dve.wait_ge(par_loaded, 96)
            link(dve.tensor_tensor(bn_scale, par2[:, 1, :], bn_rstd, ALU.mult))
            link(dve.scalar_tensor_tensor(out=gn_shift, in0=gn_mean, scalar=-1.0, in1=gn_rstd,
                                          op0=ALU.mult, op1=ALU.mult))
            for k in range(KC):
                a = affine1[:, :, k:T * KC:KC]
                b = affine1[:, :, T * KC + k:2 * T * KC:KC]
                link(dve.tensor_scalar(a, gn_rstd.rearrange("p (g t) -> p g t", g=G), bn_scale[:, k:k + 1],
                                       1.0 / TAU, ALU.mult, ALU.mult))
                link(dve.tensor_scalar(b, gn_shift.rearrange("p (g t) -> p g t", g=G), bn_mean[:, k:k + 1],
                                       bn_scale[:, k:k + 1], ALU.subtract, ALU.mult))
                link(dve.tensor_scalar(b, b, par2[:, 2, k:k + 1], 1.0 / TAU, ALU.add, ALU.mult))
            dve.sem_inc(affine1_ready, 1)

            KEEP = 1.0 - 1.0 / TAU

            def lif1(g, r):
                flat = [x_ring[:, r, t, :, :].rearrange("p k n -> p (k n)") for t in range(T)]
                n = 0
                for t in range(T - 1):
                    if t == 0:
                        wait_first(dve, "dve", y_act, g * T + 1)
                        wait_first(dve, "dve", y_pool, g * T + 1)
                    dve.scalar_tensor_tensor(out=lif1_state, in0=flat[t], scalar=1.0, in1=flat[t],
                                             op0=ALU.is_lt, op1=ALU.mult).then_inc(lif1_step, 1)
                    n += 1
                    wait_first(dve, "dve", y_act, g * T + (t + 2))
                    wait_first(dve, "dve", y_pool, g * T + (t + 2))
                    wait_first(dve, "dve", lif1_step, g * 6 + n)
                    dve.scalar_tensor_tensor(out=flat[t + 1], in0=lif1_state, scalar=KEEP, in1=flat[t + 1],
                                             op0=ALU.mult, op1=ALU.add).then_inc(lif1_step, 1)
                    n += 1
                    wait_first(dve, "dve", lif1_step, g * 6 + n)
                wait_first(dve, "dve", spikes1_turned, g + 1)
                wait_first(dve, "dve", spikes1_kept[r % 2], kept_round(g, r))
                dve.tensor_scalar(spikes1[:, r % 2, :, :].rearrange("p k (t n) -> p t k n", t=T), x_ring[:, r, :, :, :],
                                  1.0, None, ALU.is_ge, saturate=False).then_inc(spikes1_ready, 1)
                wait_first(dve, "dve", spikes1_ready, g + 1)
                dve.sem_inc(x_free, 1)

            def kept_round(g, r):
                return g * 8 - 8 * (r % 2) + 16

            dve.sem_inc(spikes1_kept[0], 16)
            dve.sem_inc(spikes1_kept[1], 16)
            with dve.Fori(0, G // XRING) as i:
                for r in range(XRING):
                    lif1(i * XRING + r, r)

            dve.wait_ge(gram_copied, KC)
            rate = tiny[:, 6, 0:KC]
            for k in range(KC):
                ins = dve.tensor_tensor(diag[:, k, :], cov[:, k, k * P:(k + 1) * P], ident[:, :], ALU.mult)
                link(ins)
            dve.sem_inc(diag_ready, 1)
            link(dve.tensor_reduce(rate, diag, AX.X, ALU.add))
            link(dve.tensor_scalar(rate, rate, 1.0 / TOKENS, None, ALU.mult))
            dve.wait_ge(rates_ready, 1)
            link(dve.tensor_scalar(rate_row, psum[:, RATE_BANK, 0:C], COVSCALE / TOKENS, None, ALU.mult))
            dve.wait_ge(blocks_copied, 2)
            for k in range(KC):
                link(dve.tensor_scalar(outer, rate_row, rate[:, k:k + 1], None, ALU.mult))
                link(dve.scalar_tensor_tensor(out=cov[:, k, 0:C], in0=cov[:, k, 0:C], scalar=COVSCALE / TOKENS,
                                              in1=outer, op0=ALU.mult, op1=ALU.subtract))
                link(dve.tensor_scalar(cov[:, k, C:CW], rate[:, k:k + 1], COVSCALE, None, ALU.mult))
            link(dve.tensor_copy(cov_hi, cov))
            link(dve.tensor_tensor(cov_lo, cov, cov_hi, ALU.subtract))
            dve.sem_inc(cov_ready, 1)
            h_var, h_mean = tiny[:, 7, :], tiny[:, 8, :]
            dve.wait_ge(w_loaded[0], 32)
            for m in range(HC):
                dve.wait_ge(wcov_ready, m + 1)
                bank = 4 + m % 4
                if m >= 2:
                    dve.wait_ge(wcov_read, 2 * m - 2)
                dve.tensor_copy(h_mean[:, m:m + 1], psum[:, bank, C:CW]).then_inc(wcov_read, 1)
                dve.tensor_tensor_reduce(prod[:, m % 2, :], psum[:, bank, 0:C], w1_again[:, m, :], 1.0, 0.0,
                                         ALU.mult, ALU.add, h_var[:, m:m + 1]).then_inc(wcov_read, 1)
            dve.wait_ge(wcov_read, 2 * HC)
            bias, gamma, beta = par1[:, 0, :], par1[:, 1, :], par1[:, 2, :]
            inv = scale1[:, 1, :]
            t2, t3, t4 = tiny[:, 2, :], tiny[:, 3, :], tiny[:, 4, :]
            for v in (h_var, h_mean):
                link(dve.tensor_tensor(v, v, inv, ALU.mult))
                link(dve.tensor_scalar(v, v, 1.0 / COVSCALE, None, ALU.mult))
            link(dve.tensor_tensor(h_mean, h_mean, bias, ALU.add))
            link(dve.tensor_scalar(t2, h_var, EPS, None, ALU.add))
            newton_rsqrt(t3, t2, t4, 3)
            link(dve.tensor_tensor(t3, t3, gamma, ALU.mult))
            link(dve.scalar_tensor_tensor(out=affine2[:, 0, :], in0=inv, scalar=1.0 / TAU, in1=t3,
                                          op0=ALU.mult, op1=ALU.mult))
            link(dve.tensor_tensor(t4, bias, h_mean, ALU.subtract))
            link(dve.tensor_tensor(t4, t4, t3, ALU.mult))
            link(dve.tensor_tensor(t4, t4, beta, ALU.add))
            link(dve.tensor_scalar(affine2[:, 1, :], t4, 1.0 / TAU, None, ALU.mult))
            dve.sem_inc(affine2_ready, 1)

            def lif2(s, q, slot):
                base = s * HP + q
                v = [hid[:, q % 2, :, t * PN:(t + 1) * PN] for t in range(T)]
                wait_first(dve, "dve", g1_read, s * G1_JOBS + 2 * (q + 1))
                n = 0
                for t in range(T - 1):
                    dve.scalar_tensor_tensor(out=lif2_state, in0=v[t], scalar=1.0, in1=v[t],
                                             op0=ALU.is_lt, op1=ALU.mult).then_inc(lif2_step, 1)
                    n += 1
                    wait_first(dve, "dve", lif2_step, base * 6 + n)
                    dve.scalar_tensor_tensor(out=v[t + 1], in0=lif2_state, scalar=KEEP, in1=v[t + 1],
                                             op0=ALU.mult, op1=ALU.add).then_inc(lif2_step, 1)
                    n += 1
                    wait_first(dve, "dve", lif2_step, base * 6 + n)
                if q == 0:
                    wait_first(dve, "dve", spikes2_free, s + 1)
                dve.tensor_scalar(spikes2[:, slot, 2 * q:2 * q + 2, :], hid[:, q % 2, :, :], 1.0, None, ALU.is_ge,
                                  saturate=False).then_inc(spikes2_ready, 1)

            def result(n, k, bank):
                wait_first(dve, "dve", g2_done, n * G2_JOBS + (k + 1))
                wait_first(dve, "dve", resid_biased, n * G2_JOBS + (k + 1))
                r = resid[:, k, :].rearrange("p (t n) -> p t n", t=T)
                dve.scalar_tensor_tensor(out=r, in0=psum[:, bank:bank + 4, 0:PN], scalar=scale2[:, 1, k:k + 1], in1=r,
                                         op0=ALU.mult, op1=ALU.add).then_inc(g2_read, 1)

            def step(s, slot, first_set):
                for k in range(KC):
                    lif2(s, 2 * k, slot)
                    lif2(s, 2 * k + 1, slot)
                    result(s - 1, k, 4 * ((first_set + 5 * k + 4) % 2))
                wait_first(dve, "dve", g2_read, s * G2_JOBS)
                dve.sem_inc(results_out, 1)

            for q in range(HP):
                lif2(0, q, 0)
            dve.sem_inc(results_out, 1)
            with dve.Fori(0, (G - 2) // 2) as i:
                for u in range(2):
                    step(i * 2 + (u + 1), (u + 1) % 2, u)
            step(G - 1, (G - 1) % 2, 0)
            for k in range(KC):
                result(G - 1, k, 4 * ((1 + k) % 2))

        @block.gpsimd
        def _(pool):
            pool.memset(ones[:, :], 1.0).then_inc(consts_set, 1)
            pool.memset(ident[:, :], 0.0).then_inc(consts_set, 1)
            pool.memset(spikes_turned[:, 0, :, :], 0.0).then_inc(zeros_set, 1)
            pool.wait_ge(consts_set, 2)
            pool.affine_select(out=ident[:, :], in_=ident[:, :], compare_op=ALU.not_equal, fill=1.0, base=0,
                               pattern=[[-1, P]], channel_multiplier=1).then_inc(consts_set, 1)
            pool.wait_ge(consts_set, 3)
            pool.tensor_copy(ident8[:, :], ident[:, :], saturate=False).then_inc(consts_set, 1)
            for q in range(9 + HC):
                pool.wait_ge(w_hi_set, 2 * (q + 1))
                if q < 9:
                    cols, at_w = 512, (slice(None), q // 3, slice((q % 3) * 512, (q % 3 + 1) * 512))
                    high, low = w1_hi[at_w], w1_lo[at_w]
                else:
                    cols, high, low = C, w2_hi[:, q - 9, :], w2_lo[:, q - 9, :]
                pool.tensor_tensor(low, w_turned[:, q % 4, 0:cols], high, ALU.subtract).then_inc(w_lo_set, 1)

            pool.wait_ge(affine1_ready, 1)
            X_ROUND = 16 * T * KC
            first = (G // XRING) * X_ROUND
            with pool.Fori(0, G // XRING) as i:
                for r in range(XRING):
                    g = i * XRING + r
                    wait_first(pool, "pool", affine1_free, g + 1)
                    pool.tensor_copy(affine1_now[:, r:r + 1, :], affine1[:, bass.ds(g, 1), :]).then_inc(affine1_copied, 1)
                    wait_first(pool, "pool", affine1_copied, g + 1)
                    wait_first(pool, "pool", x_loaded[r], i * X_ROUND + (first + X_ROUND))
                    for t in range(T):
                        for k in (1, 2):
                            e = t * KC + k
                            ins = pool.tensor_scalar(x_ring[:, r, t, k, :], x_ring[:, r, t, k, :],
                                                     affine1_now[:, r, e:e + 1],
                                                     affine1_now[:, r, T * KC + e:T * KC + e + 1], ALU.mult, ALU.add)
                        ins.then_inc(y_pool, 1)

            def bring_back(s, slot):
                pool.tensor_copy(spikes1[:, slot, :, :].rearrange("p k n -> p (k n)").bitcast(U32),
                                 spikes1_all[:, bass.ds(s * (KC * TN // 4), KC * TN // 4)]).then_inc(spikes1_back, 1)

            def add_bias(n, k):
                wait_first(pool, "pool", resid_loaded[k], n * (16 * T) + 16 * T)
                pool.tensor_scalar(resid[:, k, :], resid[:, k, :], 1.0, par2[:, 0, k:k + 1], ALU.mult, ALU.add
                                   ).then_inc(resid_biased, 1)

            for r in range(2):
                pool.wait_ge(spikes1_kept[r], 16 * (G // 2 + 1))
            pool.wait_ge(spikes1_turned, G + 2)
            bring_back(0, 0)
            bring_back(1, 1)

            def step(s, slot, more):
                for k in range(KC):
                    add_bias(s - 1, k)
                if more:
                    wait_first(pool, "pool", g1_done, s * G1_JOBS)
                    bring_back(s + 1, slot)

            with pool.Fori(0, (G - 2) // 2) as i:
                for u in range(2):
                    step(i * 2 + (u + 1), u, True)
            step(G - 1, 0, False)
            step(G, 0, False)

        @block.tensor
        def _(pe):
            pe.wait_ge(consts_set, 4)
            for q in range(9 + HC):
                if q >= 4:
                    pe.wait_ge(w_hi_set, 2 * (q - 3))
                if q < 9:
                    pe.wait_ge(w_scaled, 4 * (q % 3 + 1))
                    for i in range(4):
                        ins = pe.transpose(psum[:, q % 4, i * P:(i + 1) * P],
                                           w1_nat[:, 4 * (q % 3) + i, (q // 3) * P:(q // 3 + 1) * P], ident[:, :])
                else:
                    pe.wait_ge(w_scaled, HC + KC)
                    m = q - 9
                    for k in range(KC):
                        ins = pe.transpose(psum[:, q % 4, k * P:(k + 1) * P], w2_nat[:, k, m * P:(m + 1) * P],
                                           ident[:, :])
                ins.then_inc(w_transposed, 1)
            for n, v in enumerate((mu, tmp_a)):
                pe.wait_ge(gn_sums, 2 * n + 1)
                for k in range(KC):
                    ins = pe.matmul(psum[:, GN_BANK, 0:G * T], ones[:, :], v.rearrange("p (s k) -> p k s", k=KC)[:, k, :],
                                    start=(k == 0), stop=(k == KC - 1))
                ins.then_inc(gn_sums, 1)

            pe.wait_ge(zeros_set, 1)
            pe.wait_ge(w_hi_set, 2 * (9 + HC))
            for k in range(KC):
                ins = pe.matmul(gram[k], spikes_turned[:, 0, 0, 0:P], spikes_turned[:, 0, 1, k * P:C], start=True, stop=True)
            ins.then_inc(gram_step, STRING)
            pe.sem_inc(spikes1_turned, 2)
            pe.sem_inc(spikes2_free, 2)

            def turn(g, r, q):
                place = r * NQ + q
                wait_first(pe, "pe", turned_free, g * NQ + (q + 1))
                for i in range(2):
                    for k in range(KC):
                        o = (2 * q + i) * TOK
                        ins = pe.matmul(psum[0:TOK, 4 + 2 * (place % 2) + i, k * P:(k + 1) * P],
                                        spikes1[:, r % 2, k, o:o + TOK], ident8[:, :], start=True, stop=True)
                ins.then_inc(turned, 1)

            def add_gram(g, r, q):
                place = (r * NQ + q) % STRING
                wait_first(pe, "pe", turned_ready, g * NQ + (q + 1))
                for i in range(2):
                    for k in range(KC):
                        ins = pe.matmul(gram[k], spikes_turned[0:TOK, place, i, k * P:(k + 1) * P],
                                        spikes_turned[0:TOK, place, i, k * P:C], start=False, stop=True,
                                        skip_group_check=True)
                ins.then_inc(gram_step, 1)

            with pe.Fori(0, G // XRING) as i:
                for r in range(XRING):
                    g = i * XRING + r
                    wait_first(pe, "pe", spikes1_ready, g + 1)
                    for q in range(NQ):
                        turn(g, r, q)
                        if q >= 1:
                            add_gram(g, r, q - 1)
                    wait_first(pe, "pe", turned, (g + 1) * NQ)
                    pe.sem_inc(spikes1_turned, 1)
                    add_gram(g, r, NQ - 1)

            pe.wait_ge(gram_copied, KC)
            for i, (k, c) in enumerate(((0, 1), (0, 2), (1, 2))):
                ins = pe.transpose(psum[:, BLOCK_BANK, i * P:(i + 1) * P], cov[:, k, c * P:(c + 1) * P], ident[:, :])
            ins.then_inc(blocks_turned, 1)
            pe.wait_ge(diag_ready, 1)
            pe.wait_ge(turned_free, G * NQ + 2)
            pe.matmul(psum[:, RATE_BANK, 0:C], ones[:, :], diag.rearrange("p k c -> p (k c)"), start=True, stop=True
                      ).then_inc(rates_ready, 1)
            pe.wait_ge(cov_ready, 1)
            pe.wait_ge(w_lo_set, 9 + HC)
            for m in range(HC):
                if m >= 4:
                    pe.wait_ge(wcov_read, 2 * (m - 3))
                n = 0
                for k in range(KC):
                    for w in (w1_hi, w1_lo):
                        for cv in (cov_hi, cov_lo):
                            ins = pe.matmul(psum[:, 4 + m % 4, 0:CW], w[:, k, m * P:(m + 1) * P], cv[:, k, :],
                                            start=(n == 0), stop=(n == 4 * KC - 1))
                            n += 1
                ins.then_inc(wcov_ready, 1)

            def first_product(s, m, half, slot):
                n = 0
                for w in (w1_hi, w1_lo):
                    for k in range(KC):
                        for t in range(T):
                            ins = pe.matmul(psum[:, 4 * half + t, 0:PN], w[:, k, m * P:(m + 1) * P],
                                            spikes1[:, slot, k, t * PN:(t + 1) * PN],
                                            start=(n == 0), stop=(n == 2 * KC - 1))
                        n += 1
                ins.then_inc(g1_done, 1)

            def second_product(k, half, slot):
                n = 0
                for w in (w2_hi, w2_lo):
                    for m in range(HC):
                        for t in range(T):
                            ins = pe.matmul(psum[:, 4 * half + t, 0:PN], w[:, m, k * P:(k + 1) * P],
                                            spikes2[:, slot, m, t * PN:(t + 1) * PN],
                                            start=(n == 0), stop=(n == 2 * HC - 1))
                        n += 1
                ins.then_inc(g2_done, 1)

            pe.wait_ge(spikes1_back, 1)
            for m in range(HC):
                if m == 1:
                    pe.wait_ge(wcov_read, 2 * HC)
                if m >= 2:
                    pe.wait_ge(g1_read, m - 1)
                first_product(0, m, m % 2, 0)

            def step(s, slot, first_half):
                wait_first(pe, "pe", spikes1_back, s + 1)
                j = 0
                for k in range(KC):
                    for i in range(4):
                        m = 4 * k + i
                        if j == 0:
                            wait_first(pe, "pe", g1_read, s * G1_JOBS)
                        elif i == 1 and k > 0:
                            wait_first(pe, "pe", g2_read, (s - 1) * G2_JOBS + k)
                        elif i == 0:
                            wait_first(pe, "pe", g1_read, s * G1_JOBS + m)
                        elif j == 1:
                            wait_first(pe, "pe", results_out, s)
                        else:
                            wait_first(pe, "pe", g1_read, s * G1_JOBS + (m - 1))
                        first_product(s, m, (first_half + j) % 2, slot)
                        j += 1
                    if k == 0:
                        wait_first(pe, "pe", spikes2_ready, s * HP)
                    wait_first(pe, "pe", g1_read, s * G1_JOBS + (4 * k + 3))
                    second_product(k, (first_half + j) % 2, 1 - slot)
                    j += 1
                wait_first(pe, "pe", g2_done, s * G2_JOBS)
                pe.sem_inc(spikes2_free, 1)

            with pe.Fori(0, (G - 2) // 2) as i:
                for u in range(2):
                    step(i * 2 + (u + 1), (u + 1) % 2, u)
            step(G - 1, (G - 1) % 2, 0)
            pe.wait_ge(spikes2_ready, G * HP)
            for k in range(KC):
                if k == 0:
                    pe.wait_ge(g1_read, G * G1_JOBS)
                else:
                    pe.wait_ge(g2_read, (G - 1) * G2_JOBS + k - 1)
                second_product(k, (1 + k) % 2, (G - 1) % 2)


_INS = ["x", "L0_conv_fc1_w", "L0_conv_fc1_b", "L0_conv_fc1_gamma", "L0_conv_fc1_beta",
        "L0_conv_fc2_w", "L0_conv_fc2_b", "L0_conv_fc2_gamma", "L0_conv_fc2_beta"]


def kernel(**inputs):
    import numpy as np
    import concourse.bacc as bacc
    from concourse.bass_utils import run_bass_kernel_spmd

    nc = bacc.Bacc("TRN2", target_bir_lowering=False, num_devices=1)
    arrays, args = {}, []
    for name in _INS:
        a = np.ascontiguousarray(inputs[name])
        arrays[f"in_{name}"] = a
        args.append(nc.dram_tensor(f"in_{name}", a.shape, mybir.dt.from_np(a.dtype), kind="ExternalInput").ap())
    args.append(nc.dram_tensor("out_0", (T, B, C, N), F32, kind="ExternalOutput").ap())
    spiking_mlp(nc, *args)
    r = run_bass_kernel_spmd(nc, [arrays], core_ids=[0])
    return r.results[0]["out_0"]
```

```python
from contextlib import ExitStack

import concourse.bass as bass
from concourse import mybir

F32 = mybir.dt.float32
F16 = mybir.dt.float16
F8 = mybir.dt.float8e4
I32 = mybir.dt.int32
U32 = mybir.dt.uint32
ALU = mybir.AluOpType
ACT = mybir.ActivationFunctionType
AX = mybir.AxisListType

T, B, C, H, N = 4, 32, 384, 1536, 196
P = 128
PAIR = 2
G = B // PAIR
PN = PAIR * N
TN = T * PN
KC = C // P
HC = H // P
TOKENS = T * B * N
TAU = 1.5
EPS = 1e-5

XRING = 4
TOK = 112
NQ = TN // TOK // 2
STRING = 4
HP = HC // 2
G1_JOBS = HC
G2_JOBS = KC
COVSCALE = 16384.0


def spiking_mlp(nc, x, fc1_w, fc1_b, fc1_gamma, fc1_beta, fc2_w, fc2_b, fc2_gamma, fc2_beta, out):
    with ExitStack() as ctx:
        def sb(name, shape, dt):
            return ctx.enter_context(nc.sbuf_tensor(name, shape, dt))

        def sem(name):
            return ctx.enter_context(nc.semaphore(name))

        ctx.enter_context(nc.allow_non_contiguous_dma(reason="per-channel parameters, a few KB"))

        w1_hi = sb("w1_hi", [P, KC, H], F16)
        w1_lo = sb("w1_lo", [P, KC, H], F16)
        w2_hi = sb("w2_hi", [P, HC, C], F16)
        w2_lo = sb("w2_lo", [P, HC, C], F16)
        spikes1 = sb("spikes1", [P, 2, KC, TN], F8)
        ident = sb("ident", [P, P], F32)
        ident8 = sb("ident8", [P, P], F8)
        ones = sb("ones", [P, P], F32)
        affine1 = sb("affine1", [P, G, 2 * T * KC], F32)
        affine1_now = sb("affine1_now", [P, XRING, 2 * T * KC], F32)
        par1 = sb("par1", [P, 3, HC], F32)
        par2 = sb("par2", [P, 3, KC], F32)
        scale1 = sb("scale1", [P, 2, HC], F32)
        scale2 = sb("scale2", [P, 2, KC], F32)
        affine2 = sb("affine2", [P, 2, HC], F32)
        tiny = sb("tiny", [P, 12, HC], F32)

        spikes1_all = sb("spikes1_all", [P, G * KC * TN // 4], U32)
        early = spikes1_all[:, :].bitcast(F32)
        at = [0]

        def early_view(cols):
            at[0] += cols
            return early[:, at[0] - cols:at[0]]

        w1_nat = early_view(HC * C).rearrange("p (m c) -> p m c", m=HC)
        w2_nat = early_view(KC * H).rearrange("p (k h) -> p k h", k=KC)
        w_turned = early_view(4 * 512).rearrange("p (r n) -> p r n", r=4)
        NS = G * T * KC
        stats = early_view(NS * 6)
        mu, m2, tmp_a, tmp_b = (early_view(NS) for _ in range(4))
        gn_mean, gn_var, gn_rstd, gn_tmp, gn_shift = (early_view(G * T) for _ in range(5))

        XT = T * KC * PN
        QW = 2 * C
        ARENA = XRING * XT + KC * PN + STRING * QW // 2
        arena = sb("arena", [P, ARENA], F32)
        x_ring = arena[:, 0:XRING * XT].rearrange("p (r t b k n) -> p r t b k n", r=XRING, t=T, b=PAIR, k=KC)
        lif1_state = arena[:, XRING * XT:XRING * XT + KC * PN]
        spikes_turned = arena[:, XRING * XT + KC * PN:ARENA].bitcast(F16).rearrange(
            "p (r i c) -> p r i c", r=STRING, i=2)
        w1_again = arena[:, 0:HC * C].rearrange("p (m c) -> p m c", m=HC)
        CW = C + 1
        o = XT
        cov = arena[:, o:o + KC * CW].rearrange("p (k c) -> p k c", k=KC)
        o += KC * CW + 1
        cov_hi = arena[:, o:o + KC * 193].bitcast(F16).rearrange("p (k c) -> p k c", k=KC)[:, :, 0:CW]
        o += KC * 193
        cov_lo = arena[:, o:o + KC * 193].bitcast(F16).rearrange("p (k c) -> p k c", k=KC)[:, :, 0:CW]
        o += KC * 193
        diag = arena[:, o:o + C].rearrange("p (k c) -> p k c", k=KC)
        o += C
        rate_row = arena[:, o:o + C]
        o += C
        outer = arena[:, o:o + C]
        assert o + C <= 2 * XT
        prod = arena[:, 2 * XT:2 * XT + 2 * C].rearrange("p (r c) -> p r c", r=2)
        hid = arena[:, 0:4 * TN].rearrange("p (r m n) -> p r m n", r=2, m=2)
        o = 4 * TN
        spikes2 = arena[:, o:o + 2 * HC * TN // 4].bitcast(F8).rearrange("p (r m n) -> p r m n", r=2, m=HC)
        o += 2 * HC * TN // 4
        resid = arena[:, o:o + KC * TN].rearrange("p (u k n) -> p u k n", u=T * PAIR, k=KC)
        o += KC * TN
        lif2_state = arena[:, o:o + 2 * PN].rearrange("p (m n) -> p m n", m=2)
        assert o + 2 * PN <= ARENA

        psum = ctx.enter_context(nc.psum_tensor("psum", [P, 8, 512], F32))
        halves = psum[:, :, :].rearrange("p (f t) (b n) -> p f (t b) n", f=2, b=PAIR)[:, :, :, 0:N]
        gram = [psum[:, 0, 0:C], psum[:, 1, 0:C - P], psum[:, 2, 0:C - 2 * P]]
        GN_BANK, RATE_BANK = 7, 3

        w_loaded = [sem("w1_loaded"), sem("w2_loaded")]
        par_loaded = sem("par_loaded")
        consts_set = sem("consts_set")
        w_scales = sem("w_scales")
        w_scaled = sem("w_scaled")
        w_transposed = sem("w_transposed")
        w_hi_set = sem("w_hi_set")
        w_lo_set = sem("w_lo_set")
        x_loaded = [sem(f"x_loaded{r}") for r in range(XRING)]
        x_free = sem("x_free")
        dve_step = sem("dve_step")
        gn_sums = sem("gn_sums")
        gn_squared = sem("gn_squared")
        root_in = sem("root_in")
        root_out = sem("root_out")
        affine1_ready = sem("affine1_ready")
        affine1_copied = sem("affine1_copied")
        y_act = sem("y_act")
        y_pool = sem("y_pool")
        lif1_step = sem("lif1_step")
        spikes1_ready = sem("spikes1_ready")
        spikes1_kept = [sem(f"spikes1_kept{r}") for r in range(2)]
        turned = sem("turned")
        turned_ready = sem("turned_ready")
        gram_step = sem("gram_step")
        zeros_set = sem("zeros_set")
        diag_ready = sem("diag_ready")
        rates_ready = sem("rates_ready")
        cov_ready = sem("cov_ready")
        wcov_ready = sem("wcov_ready")
        wcov_read = sem("wcov_read")
        affine2_ready = sem("affine2_ready")
        spikes1_back = sem("spikes1_back")
        g1_done = sem("g1_done")
        g1_read = sem("g1_read")
        lif2_step = sem("lif2_step")
        spikes2_ready = sem("spikes2_ready")
        g2_done = sem("g2_done")
        g2_read = sem("g2_read")
        resid_loaded = sem("resid_loaded")
        resid_biased = sem("resid_biased")
        stored = sem("stored")
        waited = {e: sem(f"waited_{e}") for e in ("sp", "act", "dve", "pool", "pe")}

        def wait_first(eng, name, semaphore, value):
            eng.wait_ge(semaphore, value)
            if not isinstance(value, int):
                eng.sem_inc(waited[name], 1)

        def dram(a, t, g):
            return a[t, bass.ds(g * PAIR, PAIR), :, :].rearrange("b (p k) n -> p b (k n)", k=KC)

        block = ctx.enter_context(nc.Block())

        @block.sync
        def _(sp):
            def load_tile(g, r):
                for t in range(T):
                    sp.dma_start(x_ring[:, r, t, :, :, :].rearrange("p b k n -> p b (k n)"), dram(x, t, g)
                                 ).then_inc(x_loaded[r], 16)

            with sp.Fori(0, G // XRING) as i:
                for r in range(XRING):
                    wait_first(sp, "sp", x_free, i * XRING + (r + 1))
                    load_tile(i * XRING + r, r)
            for r in range(XRING):
                sp.wait_ge(x_free, G + r + 1)
                load_tile(r, r)

            def keep_spikes(g, r):
                wait_first(sp, "sp", spikes1_ready, g + 1)
                sp.dma_start(spikes1_all[:, bass.ds(g * (KC * TN // 4), KC * TN // 4)],
                             spikes1[:, r % 2, :, :].rearrange("p k n -> p (k n)").bitcast(U32)
                             ).then_inc(spikes1_kept[r % 2], 16)

            with sp.Fori(0, G // XRING - 1) as i:
                for r in range(XRING):
                    keep_spikes(i * XRING + r, r)
                    load_tile(i * XRING + (XRING + r), r)
            keep_spikes(G - XRING, 0)
            sp.dma_start(w1_again, fc1_w.rearrange("(m p) c -> p m c", p=P)).then_inc(w_loaded[0], 16)
            for r in range(1, XRING):
                keep_spikes(G - XRING + r, r)

            def load_resid(n):
                for t in range(T):
                    sp.dma_start(resid[:, t * PAIR:(t + 1) * PAIR, :, :].rearrange("p b k n -> p b (k n)"),
                                 dram(x, t, n)).then_inc(resid_loaded, 16)

            sp.wait_ge(affine2_ready, 1)
            load_resid(0)
            with sp.Fori(0, G - 1) as n:
                wait_first(sp, "sp", g2_read, n * G2_JOBS + (G2_JOBS + 1))
                for t in range(T):
                    sp.dma_start(dram(out, t, n),
                                 resid[:, t * PAIR:(t + 1) * PAIR, :, :].rearrange("p b k n -> p b (k n)")
                                 ).then_inc(stored, 16)
                wait_first(sp, "sp", stored, n * (16 * T) + 16 * T)
                load_resid(n + 1)
            for k in range(KC):
                sp.wait_ge(g2_read, (G - 1) * G2_JOBS + k + 2)
                for t in range(T):
                    sp.dma_start(out[t, (G - 1) * PAIR:G * PAIR, :, :].rearrange("b (p k) n -> p b k n", k=KC)[:, :, k, :],
                                 resid[:, t * PAIR:(t + 1) * PAIR, k, :]).then_inc(stored, 16)
            sp.wait_ge(stored, 16 * T * (G - 1 + KC))

        @block.scalar
        def _(act):
            act.dma_start(w1_nat, fc1_w.rearrange("(m p) c -> p m c", p=P)).then_inc(w_loaded[0], 16)
            act.dma_start(w2_nat, fc2_w.rearrange("(p k) h -> p k h", k=KC)).then_inc(w_loaded[1], 16)
            for i, v in enumerate((fc2_b, fc2_gamma, fc2_beta)):
                act.dma_start(par2[:, i, :], v.rearrange("(p k) -> p k", k=KC)).then_inc(par_loaded, 16)
            for i, v in enumerate((fc1_b, fc1_gamma, fc1_beta)):
                act.dma_start(par1[:, i, :], v.rearrange("(m p) -> p m", p=P)).then_inc(par_loaded, 16)
            act.wait_ge(w_scales, 1)
            for m in range(HC):
                act.activation(w1_nat[:, m, :], w1_nat[:, m, :], ACT.Copy, scale=scale1[:, 0, m:m + 1]
                               ).then_inc(w_scaled, 1)
            act.wait_ge(w_scales, 2)
            for k in range(KC):
                act.activation(w2_nat[:, k, :], w2_nat[:, k, :], ACT.Copy, scale=scale2[:, 0, k:k + 1]
                               ).then_inc(w_scaled, 1)
            for q in range(9 + HC):
                act.wait_ge(w_transposed, q + 1)
                if q >= 4:
                    act.wait_ge(w_lo_set, q - 3)
                if q < 9:
                    cols, high = 512, w1_hi[:, q // 3, (q % 3) * 512:(q % 3 + 1) * 512]
                else:
                    cols, high = C, w2_hi[:, q - 9, :]
                act.activation(w_turned[:, q % 4, 0:cols], psum[:, q % 4, 0:cols], ACT.Copy).then_inc(w_hi_set, 1)
                act.activation(high, psum[:, q % 4, 0:cols], ACT.Copy).then_inc(w_hi_set, 1)
            for n in range(2):
                act.wait_ge(root_in, n + 1)
                src, dst = ((gn_var, gn_rstd), (tiny[:, 2, 0:KC], tiny[:, 3, 0:KC]))[n]
                act.activation(dst, src, ACT.Sqrt).then_inc(root_out, 1)

            act.sem_inc(y_act, XRING * T)
            act.sem_inc(turned_ready, 2)

            def normalise(g, r, rounds):
                wait_first(act, "act", affine1_copied, g + 1)
                wait_first(act, "act", x_loaded[r], rounds)
                for t in range(T):
                    act.activation(x_ring[:, r, t, :, 0, :], x_ring[:, r, t, :, 0, :], ACT.Identity,
                                   scale=affine1_now[:, r, t * KC:t * KC + 1],
                                   bias=affine1_now[:, r, T * KC + t * KC:T * KC + t * KC + 1]).then_inc(y_act, 1)

            def turn_out(g, r):
                for q in range(NQ):
                    place = (r * NQ + q)
                    wait_first(act, "act", turned, g * NQ + (q + 1 + 2 * NQ))
                    wait_first(act, "act", gram_step, g * NQ + (q + 1))
                    s = 4 + 2 * (place % 2)
                    act.activation(spikes_turned[0:TOK, place % STRING, :, :], psum[0:TOK, s:s + 2, 0:C], ACT.Copy
                                   ).then_inc(turned_ready, 1)

            X_ROUND = 16 * T
            first = (G // XRING) * X_ROUND
            normalise(0, 0, first + X_ROUND)
            with act.Fori(0, G // XRING - 1) as i:
                for r in range(XRING):
                    normalise(i * XRING + (r + 1), (r + 1) % XRING,
                              i * X_ROUND + (first + (2 if r == XRING - 1 else 1) * X_ROUND))
                    turn_out(i * XRING + r, r)
            for r in range(XRING):
                if r < XRING - 1:
                    normalise(G - XRING + r + 1, r + 1, 2 * first)
                turn_out(G - XRING + r, r)

            act.wait_ge(root_in, 3)
            act.activation(tiny[:, 3, :], tiny[:, 2, :], ACT.Sqrt).then_inc(root_out, 1)

            def hidden(s, m):
                wait_first(act, "act", g1_done, s * G1_JOBS + (m + 1))
                if isinstance(s, int) and s * HP + m // 2 < 2:
                    pass
                else:
                    wait_first(act, "act", spikes2_ready, s * HP + (m // 2 - 1))
                act.activation(hid[:, (m // 2) % 2, m % 2, :].rearrange("p (u n) -> p u n", n=N),
                               halves[:, job_half(s, m), :, :], ACT.Identity,
                               scale=affine2[:, 0, m:m + 1], bias=affine2[:, 1, m:m + 1]).then_inc(g1_read, 1)

            def job_half(s, m):
                if isinstance(s, int) and s == 0:
                    return m % 2
                return (m + m // 4 + parity[0]) % 2

            parity = [0]
            act.wait_ge(affine2_ready, 1)
            for m in range(HC):
                hidden(0, m)
            with act.Fori(0, (G - 2) // 2) as i:
                for u in range(2):
                    parity[0] = u
                    for m in range(HC):
                        hidden(i * 2 + (u + 1), m)
            parity[0] = 0
            for m in range(HC):
                hidden(G - 1, m)

        @block.vector
        def _(dve):
            count = [0]

            def link(ins):
                count[0] += 1
                ins.then_inc(dve_step, 1)
                dve.wait_ge(dve_step, count[0])

            dve.sem_inc(x_free, XRING)
            for n, (w, sc, rows) in enumerate(((w1_nat, scale1, HC), (w2_nat, scale2, KC))):
                dve.wait_ge(w_loaded[n], 16)
                big = tiny[:, 0, 0:rows]
                least = tiny[:, 1, 0:rows]
                link(dve.tensor_reduce(big, w, AX.X, ALU.max))
                link(dve.tensor_reduce(least, w, AX.X, ALU.min))
                link(dve.scalar_tensor_tensor(out=big, in0=least, scalar=-1.0, in1=big, op0=ALU.mult, op1=ALU.max))
                link(dve.tensor_scalar(big, big, 2.0 ** -100, None, ALU.max))
                expo = tiny[:, 1, 0:rows].bitcast(I32)
                link(dve.tensor_scalar(expo, big.bitcast(I32), 0x7F800000, None, ALU.bitwise_and))
                link(dve.tensor_scalar(sc[:, 0, :].bitcast(I32), expo, -1.0, float(268 << 23), ALU.mult, ALU.add))
                link(dve.tensor_scalar(sc[:, 1, :].bitcast(I32), expo, float(-(14 << 23)), None, ALU.add))
                dve.sem_inc(w_scales, 1)

            with dve.Fori(0, G // XRING) as i:
                for r in range(XRING):
                    wait_first(dve, "dve", x_loaded[r], i * (16 * T) + 16 * T)
                    for e in range(T * KC):
                        ins = dve.bn_stats(stats[:, bass.ds((i * XRING + r) * (6 * T * KC) + 6 * e, 6)],
                                           x_ring[:, r, e // KC, :, e % KC, :])
                    ins.then_inc(x_free, 1)
            dve.wait_ge(x_free, G + XRING)

            st = stats.rearrange("p (s v) -> p v s", v=6)
            link(dve.tensor_tensor(mu, st[:, 1, :], st[:, 4, :], ALU.add))
            link(dve.tensor_scalar(mu, mu, 0.5, None, ALU.mult))
            link(dve.tensor_tensor(tmp_a, st[:, 1, :], st[:, 4, :], ALU.subtract))
            link(dve.tensor_tensor(tmp_a, tmp_a, tmp_a, ALU.mult))
            link(dve.tensor_tensor(m2, st[:, 2, :], st[:, 5, :], ALU.add))
            link(dve.scalar_tensor_tensor(out=m2, in0=tmp_a, scalar=PN / 4.0, in1=m2, op0=ALU.mult, op1=ALU.add))
            link(dve.tensor_scalar(m2, m2, 1.0 / PN, None, ALU.mult))

            def by_chunk(v):
                return v.rearrange("p (s k) -> p s k", k=KC)

            def over_chunks(v):
                return v.unsqueeze(2).to_broadcast([P, G * T, KC])

            def over_slots(v):
                return v.unsqueeze(1).to_broadcast([P, G * T, KC])

            def newton_rsqrt(dst, var, tmp, n):
                dve.sem_inc(root_in, 1)
                dve.wait_ge(root_out, n)
                link(dve.reciprocal(dst, dst))
                link(dve.tensor_tensor(tmp, dst, dst, ALU.mult))
                link(dve.tensor_tensor(tmp, tmp, var, ALU.mult))
                link(dve.tensor_scalar(tmp, tmp, -0.5, 1.5, ALU.mult, ALU.add))
                link(dve.tensor_tensor(dst, dst, tmp, ALU.mult))

            dve.sem_inc(gn_sums, 1)
            sums = psum[:, GN_BANK, 0:G * T]
            dve.wait_ge(gn_sums, 2)
            link(dve.tensor_scalar(gn_mean, sums, 1.0 / C, None, ALU.mult))
            link(dve.tensor_tensor(by_chunk(mu), by_chunk(mu), over_chunks(gn_mean), ALU.subtract))
            link(dve.tensor_tensor(tmp_a, mu, mu, ALU.mult))
            link(dve.tensor_tensor(tmp_a, tmp_a, m2, ALU.add))
            dve.sem_inc(gn_sums, 1)
            dve.wait_ge(gn_sums, 4)
            link(dve.tensor_scalar(gn_var, sums, 1.0 / C, EPS, ALU.mult, ALU.add))
            newton_rsqrt(gn_rstd, gn_var, gn_tmp, 1)
            link(dve.tensor_tensor(by_chunk(mu), by_chunk(mu), over_chunks(gn_rstd), ALU.mult))
            bn_mean, bn_var, bn_rstd, bn_tmp, bn_scale = (tiny[:, i, 0:KC] for i in (1, 2, 3, 4, 5))
            link(dve.tensor_reduce(bn_mean, mu.rearrange("p (s k) -> p k s", k=KC), AX.X, ALU.add))
            link(dve.tensor_scalar(bn_mean, bn_mean, 1.0 / (G * T), None, ALU.mult))
            dve.tensor_tensor(gn_tmp, gn_rstd, gn_rstd, ALU.mult).then_inc(gn_squared, 1)
            link(dve.tensor_tensor(by_chunk(tmp_a), by_chunk(mu), over_slots(bn_mean), ALU.subtract))
            dve.wait_ge(gn_squared, 1)
            link(dve.tensor_tensor(by_chunk(tmp_b), by_chunk(m2), over_chunks(gn_tmp), ALU.mult))
            link(dve.tensor_tensor(tmp_a, tmp_a, tmp_a, ALU.mult))
            link(dve.tensor_tensor(tmp_a, tmp_a, tmp_b, ALU.add))
            link(dve.tensor_reduce(bn_var, tmp_a.rearrange("p (s k) -> p k s", k=KC), AX.X, ALU.add))
            link(dve.tensor_scalar(bn_var, bn_var, 1.0 / (G * T), EPS, ALU.mult, ALU.add))
            newton_rsqrt(bn_rstd, bn_var, bn_tmp, 2)
            dve.wait_ge(par_loaded, 96)
            link(dve.tensor_tensor(bn_scale, par2[:, 1, :], bn_rstd, ALU.mult))
            link(dve.scalar_tensor_tensor(out=gn_shift, in0=gn_mean, scalar=-1.0, in1=gn_rstd,
                                          op0=ALU.mult, op1=ALU.mult))
            for k in range(KC):
                a = affine1[:, :, k:T * KC:KC]
                b = affine1[:, :, T * KC + k:2 * T * KC:KC]
                link(dve.tensor_scalar(a, gn_rstd.rearrange("p (g t) -> p g t", g=G), bn_scale[:, k:k + 1],
                                       1.0 / TAU, ALU.mult, ALU.mult))
                link(dve.tensor_scalar(b, gn_shift.rearrange("p (g t) -> p g t", g=G), bn_mean[:, k:k + 1],
                                       bn_scale[:, k:k + 1], ALU.subtract, ALU.mult))
                link(dve.tensor_scalar(b, b, par2[:, 2, k:k + 1], 1.0 / TAU, ALU.add, ALU.mult))
            dve.sem_inc(affine1_ready, 1)

            KEEP = 1.0 - 1.0 / TAU

            HALF = KC * N

            def lif1(g, r):
                flat = [[x_ring[:, r, t, b, :, :].rearrange("p k n -> p (k n)") for b in range(PAIR)] for t in range(T)]
                state = [lif1_state[:, b * HALF:(b + 1) * HALF] for b in range(PAIR)]
                per_tile = 2 * PAIR * (T - 1)
                n = 0
                for t in range(T - 1):
                    if t == 0:
                        wait_first(dve, "dve", y_act, g * T + (1 + XRING * T))
                        wait_first(dve, "dve", y_pool, g * T + 1)
                    for b in range(PAIR):
                        if t > 0:
                            wait_first(dve, "dve", lif1_step, g * per_tile + (n - 1))
                        dve.scalar_tensor_tensor(out=state[b], in0=flat[t][b], scalar=1.0, in1=flat[t][b],
                                                 op0=ALU.is_lt, op1=ALU.mult).then_inc(lif1_step, 1)
                        n += 1
                    wait_first(dve, "dve", y_act, g * T + (t + 2 + XRING * T))
                    wait_first(dve, "dve", y_pool, g * T + (t + 2))
                    for b in range(PAIR):
                        wait_first(dve, "dve", lif1_step, g * per_tile + (n - 1))
                        dve.scalar_tensor_tensor(out=flat[t + 1][b], in0=state[b], scalar=KEEP, in1=flat[t + 1][b],
                                                 op0=ALU.mult, op1=ALU.add).then_inc(lif1_step, 1)
                        n += 1
                wait_first(dve, "dve", lif1_step, g * per_tile + n)
                wait_first(dve, "dve", turned, (g + 1) * NQ)
                wait_first(dve, "dve", spikes1_kept[r % 2], kept_round(g, r))
                dve.tensor_scalar(spikes1[:, r % 2, :, :].rearrange("p k (u n) -> p u k n", n=N),
                                  x_ring[:, r, :, :, :, :].rearrange("p t b k n -> p (t b) k n"),
                                  1.0, None, ALU.is_ge, saturate=False).then_inc(spikes1_ready, 1)

            def kept_round(g, r):
                return g * 8 - 8 * (r % 2) + 16

            dve.sem_inc(g2_read, 1)
            dve.sem_inc(spikes1_kept[0], 16)
            dve.sem_inc(spikes1_kept[1], 16)
            with dve.Fori(0, G // XRING) as i:
                for r in range(XRING):
                    lif1(i * XRING + r, r)

            dve.wait_ge(gram_step, G * NQ + STRING)
            rate = tiny[:, 6, 0:KC]
            for k in range(KC):
                dve.tensor_tensor(diag[:, k, :], gram[k][:, 0:P], ident[:, :], ALU.mult).then_inc(diag_ready, 1)
            dve.wait_ge(diag_ready, KC)
            link(dve.tensor_reduce(rate, diag, AX.X, ALU.add))
            link(dve.tensor_scalar(rate, rate, 1.0 / TOKENS, None, ALU.mult))
            dve.wait_ge(rates_ready, 1)
            link(dve.tensor_scalar(rate_row, psum[:, RATE_BANK, 0:C], COVSCALE / TOKENS, None, ALU.mult))
            for k in range(KC):
                link(dve.tensor_scalar(outer[:, k * P:C], rate_row[:, k * P:C], rate[:, k:k + 1], None, ALU.mult))
                if k < KC - 1:
                    dve.tensor_scalar(cov[:, k, C:CW], rate[:, k:k + 1], COVSCALE, None, ALU.mult)
                    link(dve.scalar_tensor_tensor(out=cov[:, k, k * P:C], in0=gram[k], scalar=COVSCALE / TOKENS,
                                                  in1=outer[:, k * P:C], op0=ALU.mult, op1=ALU.subtract))
                    link(dve.tensor_scalar(cov[:, k, (k + 1) * P:C], cov[:, k, (k + 1) * P:C], 2.0, None, ALU.mult))
                else:
                    dve.tensor_scalar(cov[:, k, C:CW], rate[:, k:k + 1], COVSCALE, None, ALU.mult)
                    link(dve.scalar_tensor_tensor(out=cov[:, k, k * P:C], in0=gram[k], scalar=COVSCALE / TOKENS,
                                                  in1=outer[:, k * P:C], op0=ALU.mult, op1=ALU.subtract))
                link(dve.tensor_copy(cov_hi[:, k, k * P:CW], cov[:, k, k * P:CW]))
                dve.tensor_tensor(cov_lo[:, k, k * P:CW], cov[:, k, k * P:CW], cov_hi[:, k, k * P:CW], ALU.subtract
                                  ).then_inc(cov_ready, 1)
            h_var, h_mean = tiny[:, 7, :], tiny[:, 8, :]
            dve.wait_ge(w_loaded[0], 32)
            for m in range(HC):
                dve.wait_ge(wcov_ready, m + 1)
                bank = 4 + m % 4
                if m >= 2:
                    dve.wait_ge(wcov_read, 2 * m - 2)
                dve.tensor_copy(h_mean[:, m:m + 1], psum[:, bank, C:CW]).then_inc(wcov_read, 1)
                dve.tensor_tensor_reduce(prod[:, m % 2, :].rearrange("p (k c) -> p k c", k=KC),
                                         psum[:, bank, 0:C].rearrange("p (k c) -> p k c", k=KC),
                                         w1_again[:, m, :].rearrange("p (c k) -> p k c", k=KC), 1.0, 0.0,
                                         ALU.mult, ALU.add, h_var[:, m:m + 1]).then_inc(wcov_read, 1)
            dve.wait_ge(wcov_read, 2 * HC)
            bias, gamma, beta = par1[:, 0, :], par1[:, 1, :], par1[:, 2, :]
            inv = scale1[:, 1, :]
            t2, t3, t4 = tiny[:, 2, :], tiny[:, 3, :], tiny[:, 4, :]
            for v in (h_var, h_mean):
                link(dve.tensor_tensor(v, v, inv, ALU.mult))
                link(dve.tensor_scalar(v, v, 1.0 / COVSCALE, None, ALU.mult))
            link(dve.tensor_tensor(h_mean, h_mean, bias, ALU.add))
            link(dve.tensor_scalar(t2, h_var, EPS, None, ALU.add))
            newton_rsqrt(t3, t2, t4, 3)
            link(dve.tensor_tensor(t3, t3, gamma, ALU.mult))
            link(dve.scalar_tensor_tensor(out=affine2[:, 0, :], in0=inv, scalar=1.0 / TAU, in1=t3,
                                          op0=ALU.mult, op1=ALU.mult))
            link(dve.tensor_tensor(t4, bias, h_mean, ALU.subtract))
            link(dve.tensor_tensor(t4, t4, t3, ALU.mult))
            link(dve.tensor_tensor(t4, t4, beta, ALU.add))
            link(dve.tensor_scalar(affine2[:, 1, :], t4, 1.0 / TAU, None, ALU.mult))
            dve.sem_inc(affine2_ready, 1)

            def lif2(s, q, slot):
                base = s * HP + q
                v = [hid[:, q % 2, :, t * PN:(t + 1) * PN] for t in range(T)]
                wait_first(dve, "dve", g1_read, s * G1_JOBS + 2 * (q + 1))
                n = 0
                for t in range(T - 1):
                    dve.scalar_tensor_tensor(out=lif2_state, in0=v[t], scalar=1.0, in1=v[t],
                                             op0=ALU.is_lt, op1=ALU.mult).then_inc(lif2_step, 1)
                    n += 1
                    wait_first(dve, "dve", lif2_step, base * 6 + n)
                    dve.scalar_tensor_tensor(out=v[t + 1], in0=lif2_state, scalar=KEEP, in1=v[t + 1],
                                             op0=ALU.mult, op1=ALU.add).then_inc(lif2_step, 1)
                    n += 1
                    wait_first(dve, "dve", lif2_step, base * 6 + n)
                if q == 0 and not (isinstance(s, int) and s < 2):
                    wait_first(dve, "dve", g2_done, (s - 1) * G2_JOBS + 1)
                dve.tensor_scalar(spikes2[:, slot, 2 * q:2 * q + 2, :], hid[:, q % 2, :, :], 1.0, None, ALU.is_ge,
                                  saturate=False).then_inc(spikes2_ready, 1)

            def result(n, k, half):
                wait_first(dve, "dve", g2_done, n * G2_JOBS + (k + 2))
                wait_first(dve, "dve", resid_biased, n * G2_JOBS + (k + 1))
                dve.scalar_tensor_tensor(out=resid[:, :, k, :], in0=halves[:, half, :, :], scalar=scale2[:, 1, k:k + 1],
                                         in1=resid[:, :, k, :], op0=ALU.mult, op1=ALU.add).then_inc(g2_read, 1)

            def step(s, slot, first_half):
                for k in range(KC):
                    lif2(s, 2 * k, slot)
                    lif2(s, 2 * k + 1, slot)
                    result(s - 1, k, (first_half + 5 * k + 4) % 2)

            for q in range(HP):
                lif2(0, q, 0)
            with dve.Fori(0, (G - 2) // 2) as i:
                for u in range(2):
                    step(i * 2 + (u + 1), (u + 1) % 2, u)
            step(G - 1, (G - 1) % 2, 0)
            for k in range(KC):
                result(G - 1, k, (1 + k) % 2)

        @block.gpsimd
        def _(pool):
            pool.memset(ones[:, :], 1.0).then_inc(consts_set, 1)
            pool.memset(ident[:, :], 0.0).then_inc(consts_set, 1)
            pool.memset(spikes_turned[:, 0, :, :], 0.0).then_inc(zeros_set, 1)
            pool.wait_ge(consts_set, 2)
            pool.affine_select(out=ident[:, :], in_=ident[:, :], compare_op=ALU.not_equal, fill=1.0, base=0,
                               pattern=[[-1, P]], channel_multiplier=1).then_inc(consts_set, 1)
            pool.wait_ge(consts_set, 3)
            pool.tensor_copy(ident8[:, :], ident[:, :], saturate=False).then_inc(consts_set, 1)
            for q in range(9 + HC):
                pool.wait_ge(w_hi_set, 2 * (q + 1))
                if q < 9:
                    cols, at_w = 512, (slice(None), q // 3, slice((q % 3) * 512, (q % 3 + 1) * 512))
                    high, low = w1_hi[at_w], w1_lo[at_w]
                else:
                    cols, high, low = C, w2_hi[:, q - 9, :], w2_lo[:, q - 9, :]
                pool.tensor_tensor(low, w_turned[:, q % 4, 0:cols], high, ALU.subtract).then_inc(w_lo_set, 1)

            pool.wait_ge(affine1_ready, 1)
            X_ROUND = 16 * T
            first = (G // XRING) * X_ROUND
            with pool.Fori(0, G // XRING) as i:
                for r in range(XRING):
                    g = i * XRING + r
                    wait_first(pool, "pool", y_act, (g + 1) * T)
                    pool.tensor_copy(affine1_now[:, r:r + 1, :], affine1[:, bass.ds(g, 1), :]).then_inc(affine1_copied, 1)
                    wait_first(pool, "pool", affine1_copied, g + 1)
                    wait_first(pool, "pool", x_loaded[r], i * X_ROUND + (first + X_ROUND))
                    for t in range(T):
                        for k in (1, 2):
                            e = t * KC + k
                            ins = pool.tensor_scalar(x_ring[:, r, t, :, k, :], x_ring[:, r, t, :, k, :],
                                                     affine1_now[:, r, e:e + 1],
                                                     affine1_now[:, r, T * KC + e:T * KC + e + 1], ALU.mult, ALU.add)
                        ins.then_inc(y_pool, 1)

            def bring_back(s, slot):
                pool.tensor_copy(spikes1[:, slot, :, :].rearrange("p k n -> p (k n)").bitcast(U32),
                                 spikes1_all[:, bass.ds(s * (KC * TN // 4), KC * TN // 4)]).then_inc(spikes1_back, 1)

            def add_bias(n, k):
                wait_first(pool, "pool", resid_loaded, n * (16 * T) + 16 * T)
                pool.tensor_scalar(resid[:, :, k, :], resid[:, :, k, :], 1.0, par2[:, 0, k:k + 1], ALU.mult, ALU.add
                                   ).then_inc(resid_biased, 1)

            for r in range(2):
                pool.wait_ge(spikes1_kept[r], 16 * (G // 2 + 1))
            pool.wait_ge(turned, (G + 2) * NQ)
            bring_back(0, 0)
            bring_back(1, 1)

            def step(s, slot, more):
                for k in range(KC):
                    add_bias(s - 1, k)
                if more:
                    wait_first(pool, "pool", g1_done, s * G1_JOBS)
                    bring_back(s + 1, slot)

            with pool.Fori(0, (G - 2) // 2) as i:
                for u in range(2):
                    step(i * 2 + (u + 1), u, True)
            step(G - 1, 0, False)
            step(G, 0, False)

        @block.tensor
        def _(pe):
            pe.wait_ge(consts_set, 4)
            for q in range(9 + HC):
                if q >= 4:
                    pe.wait_ge(w_hi_set, 2 * (q - 3))
                if q < 9:
                    pe.wait_ge(w_scaled, 4 * (q % 3 + 1))
                    for i in range(4):
                        ins = pe.transpose(psum[:, q % 4, i * P:(i + 1) * P],
                                           w1_nat[:, 4 * (q % 3) + i, q // 3:C:KC], ident[:, :])
                else:
                    pe.wait_ge(w_scaled, HC + KC)
                    m = q - 9
                    for k in range(KC):
                        ins = pe.transpose(psum[:, q % 4, k * P:(k + 1) * P], w2_nat[:, k, m * P:(m + 1) * P],
                                           ident[:, :])
                ins.then_inc(w_transposed, 1)
            for n, v in enumerate((mu, tmp_a)):
                pe.wait_ge(gn_sums, 2 * n + 1)
                for k in range(KC):
                    ins = pe.matmul(psum[:, GN_BANK, 0:G * T], ones[:, :], v.rearrange("p (s k) -> p k s", k=KC)[:, k, :],
                                    start=(k == 0), stop=(k == KC - 1))
                ins.then_inc(gn_sums, 1)

            pe.wait_ge(zeros_set, 1)
            pe.wait_ge(w_hi_set, 2 * (9 + HC))
            for k in range(KC):
                ins = pe.matmul(gram[k], spikes_turned[:, 0, 0, 0:P], spikes_turned[:, 0, 1, k * P:C], start=True, stop=True)
            ins.then_inc(gram_step, STRING)
            pe.sem_inc(turned, 2 * NQ)
            pe.sem_inc(g2_done, 1)

            def turn(g, r, q):
                place = r * NQ + q
                wait_first(pe, "pe", turned_ready, g * NQ + (q + 1))
                for i in range(2):
                    for k in range(KC):
                        o = (2 * q + i) * TOK
                        ins = pe.matmul(psum[0:TOK, 4 + 2 * (place % 2) + i, k * P:(k + 1) * P],
                                        spikes1[:, r % 2, k, o:o + TOK], ident8[:, :], start=True, stop=True)
                ins.then_inc(turned, 1)

            def add_gram(g, r, q):
                place = (r * NQ + q) % STRING
                wait_first(pe, "pe", turned_ready, g * NQ + (q + 3))
                for i in range(2):
                    for k in range(KC):
                        ins = pe.matmul(gram[k], spikes_turned[0:TOK, place, i, k * P:(k + 1) * P],
                                        spikes_turned[0:TOK, place, i, k * P:C], start=False, stop=True,
                                        skip_group_check=True)
                ins.then_inc(gram_step, 1)

            with pe.Fori(0, G // XRING) as i:
                for r in range(XRING):
                    g = i * XRING + r
                    wait_first(pe, "pe", spikes1_ready, g + 1)
                    for q in range(NQ):
                        turn(g, r, q)
                        if q >= 1:
                            add_gram(g, r, q - 1)
                    add_gram(g, r, NQ - 1)

            pe.wait_ge(diag_ready, KC)
            pe.matmul(psum[:, RATE_BANK, 0:C], ones[:, :], diag.rearrange("p k c -> p (k c)"), start=True, stop=True
                      ).then_inc(rates_ready, 1)
            pe.wait_ge(w_lo_set, 9 + HC)
            pe.wait_ge(turned_ready, G * NQ + 2)
            for m in range(HC):
                if m >= 4:
                    pe.wait_ge(wcov_read, 2 * (m - 3))
                for k in range(KC):
                    if m == 0:
                        pe.wait_ge(cov_ready, k + 1)
                    for w in (w1_hi, w1_lo):
                        for cv in (cov_hi, cov_lo):
                            ins = pe.matmul(psum[:, 4 + m % 4, k * P:CW], w[:, k, m * P:(m + 1) * P], cv[:, k, k * P:CW],
                                            start=(k == 0 and w is w1_hi and cv is cov_hi), stop=(k == KC - 1),
                                            skip_group_check=True)
                ins.then_inc(wcov_ready, 1)

            def first_product(s, m, half, slot):
                n = 0
                for w in (w1_hi, w1_lo):
                    for k in range(KC):
                        for t in range(T):
                            ins = pe.matmul(halves[:, half, t * PAIR:(t + 1) * PAIR, :], w[:, k, m * P:(m + 1) * P],
                                            spikes1[:, slot, k, t * PN:(t + 1) * PN],
                                            start=(n == 0), stop=(n == 2 * KC - 1))
                        n += 1
                ins.then_inc(g1_done, 1)

            def second_product(k, half, slot):
                n = 0
                for w in (w2_hi, w2_lo):
                    for m in range(HC):
                        for t in range(T):
                            ins = pe.matmul(halves[:, half, t * PAIR:(t + 1) * PAIR, :], w[:, m, k * P:(k + 1) * P],
                                            spikes2[:, slot, m, t * PN:(t + 1) * PN],
                                            start=(n == 0), stop=(n == 2 * HC - 1))
                        n += 1
                ins.then_inc(g2_done, 1)

            pe.wait_ge(spikes1_back, 1)
            for m in range(HC):
                if m == 1:
                    pe.wait_ge(wcov_read, 2 * HC)
                if m >= 2:
                    pe.wait_ge(g1_read, m - 1)
                first_product(0, m, m % 2, 0)

            def step(s, slot, first_half):
                wait_first(pe, "pe", spikes1_back, s + 1)
                j = 0
                for k in range(KC):
                    for i in range(4):
                        m = 4 * k + i
                        if j == 0:
                            wait_first(pe, "pe", g1_read, s * G1_JOBS)
                        elif i == 1 and k > 0:
                            wait_first(pe, "pe", g2_read, (s - 1) * G2_JOBS + (k + 1))
                        elif i == 0:
                            wait_first(pe, "pe", g1_read, s * G1_JOBS + m)
                        elif j == 1:
                            wait_first(pe, "pe", g2_read, (s - 1) * G2_JOBS + 1)
                        else:
                            wait_first(pe, "pe", g1_read, s * G1_JOBS + (m - 1))
                        first_product(s, m, (first_half + j) % 2, slot)
                        j += 1
                    if k == 0:
                        wait_first(pe, "pe", spikes2_ready, s * HP)
                    wait_first(pe, "pe", g1_read, s * G1_JOBS + (4 * k + 3))
                    second_product(k, (first_half + j) % 2, 1 - slot)
                    j += 1

            with pe.Fori(0, (G - 2) // 2) as i:
                for u in range(2):
                    step(i * 2 + (u + 1), (u + 1) % 2, u)
            step(G - 1, (G - 1) % 2, 0)
            pe.wait_ge(spikes2_ready, G * HP)
            for k in range(KC):
                if k == 0:
                    pe.wait_ge(g1_read, G * G1_JOBS)
                else:
                    pe.wait_ge(g2_read, (G - 1) * G2_JOBS + k)
                second_product(k, (1 + k) % 2, (G - 1) % 2)


_INS = ["x", "L0_conv_fc1_w", "L0_conv_fc1_b", "L0_conv_fc1_gamma", "L0_conv_fc1_beta",
        "L0_conv_fc2_w", "L0_conv_fc2_b", "L0_conv_fc2_gamma", "L0_conv_fc2_beta"]


def kernel(**inputs):
    import numpy as np
    import concourse.bacc as bacc
    from concourse.bass_utils import run_bass_kernel_spmd

    nc = bacc.Bacc("TRN2", target_bir_lowering=False, num_devices=1)
    arrays, args = {}, []
    for name in _INS:
        a = np.ascontiguousarray(inputs[name])
        arrays[f"in_{name}"] = a
        args.append(nc.dram_tensor(f"in_{name}", a.shape, mybir.dt.from_np(a.dtype), kind="ExternalInput").ap())
    args.append(nc.dram_tensor("out_0", (T, B, C, N), F32, kind="ExternalOutput").ap())
    spiking_mlp(nc, *args)
    r = run_bass_kernel_spmd(nc, [arrays], core_ids=[0])
    return r.results[0]["out_0"]
```

```python
from contextlib import ExitStack

import concourse.bass as bass
from concourse import mybir

F32 = mybir.dt.float32
F16 = mybir.dt.float16
F8 = mybir.dt.float8e4
I32 = mybir.dt.int32
U32 = mybir.dt.uint32
ALU = mybir.AluOpType
ACT = mybir.ActivationFunctionType
AX = mybir.AxisListType

T, B, C, H, N = 4, 32, 384, 1536, 196
P = 128
PAIR = 2
G = B // PAIR
PN = PAIR * N
TN = T * PN
KC = C // P
HC = H // P
TOKENS = T * B * N
TAU = 1.5
EPS = 1e-5

XRING = 4
TOK = 112
NQ = TN // TOK // 2
KEPT_AFTER = (1, 3, 5, 6)
STRING = 4
SPIKE_WORDS = KC * TN // 4
AHEAD = 2
BY_TIME = 2
FIRST_KEPT = 1
HP = HC // 2
G1_JOBS = HC
G2_JOBS = KC
COVSCALE = 16384.0


def spiking_mlp(nc, x, fc1_w, fc1_b, fc1_gamma, fc1_beta, fc2_w, fc2_b, fc2_gamma, fc2_beta, out):
    with ExitStack() as ctx:
        def sb(name, shape, dt):
            return ctx.enter_context(nc.sbuf_tensor(name, shape, dt))

        def sem(name):
            return ctx.enter_context(nc.semaphore(name))

        ctx.enter_context(nc.allow_non_contiguous_dma(reason="per-channel parameters, a few KB"))

        w1_hi = sb("w1_hi", [P, KC, H], F16)
        w1_lo = sb("w1_lo", [P, KC, H], F16)
        w2_hi = sb("w2_hi", [P, HC, C], F16)
        w2_lo = sb("w2_lo", [P, HC, C], F16)
        spikes1 = sb("spikes1", [P, 2, KC, TN], F8)
        ident = sb("ident", [P, P], F32)
        ident8 = sb("ident8", [P, P], F8)
        ones = sb("ones", [P, P], F32)
        affine1 = sb("affine1", [P, G, 2 * T * KC], F32)
        affine1_now = sb("affine1_now", [P, XRING, 2 * T * KC], F32)
        par1 = sb("par1", [P, 3, HC], F32)
        par2 = sb("par2", [P, 3, KC], F32)
        scale1 = sb("scale1", [P, 2, HC], F32)
        scale2 = sb("scale2", [P, 2, KC], F32)
        affine2 = sb("affine2", [P, 2, HC], F32)
        tiny = sb("tiny", [P, 12, HC], F32)

        spikes1_all = sb("spikes1_all", [P, G * KC * TN // 4], U32)
        early = spikes1_all[:, :].bitcast(F32)
        at = [0]

        def early_view(cols):
            at[0] += cols
            return early[:, at[0] - cols:at[0]]

        w1_nat = early_view(HC * C).rearrange("p (m c) -> p m c", m=HC)
        w2_nat = early_view(KC * H).rearrange("p (k h) -> p k h", k=KC)
        w_turned = early_view(4 * 512).rearrange("p (r n) -> p r n", r=4)
        NS = G * T * KC
        stats = early_view(NS * 6)
        mu, m2, tmp_a, tmp_b = (early_view(NS) for _ in range(4))
        gn_mean, gn_var, gn_rstd, gn_tmp, gn_shift = (early_view(G * T) for _ in range(5))

        spikes_tile0 = spikes1_all[:, 0:SPIKE_WORDS].bitcast(F8).rearrange("p (k n) -> p k n", k=KC)
        late = spikes1_all[:, (G - 2) * SPIKE_WORDS:G * SPIKE_WORDS]
        w_stage = late[:, 0:2 * 2 * C // 2].bitcast(F16).rearrange("p (r w k m) -> p r w k m", r=2, w=2, k=KC)
        h_stage = late[:, 2 * C:2 * C + TN].bitcast(F32)
        spikes2_last = spikes1_all[:, 0:HC * TN // 4].bitcast(F8).rearrange("p (m n) -> p m n", m=HC)
        KEPT_RING = 4
        hid_last = spikes1_all[:, HC * TN // 4:HC * TN // 4 + KEPT_RING * 2 * TN].bitcast(F32).rearrange(
            "p (r m n) -> p r m n", r=KEPT_RING, m=2)
        h_kept = nc.dram_tensor("h_kept", (HC, P, TN), F32, kind="Internal").ap()

        XT = T * KC * PN
        QW = 2 * C
        ARENA = XRING * XT + KC * PN + STRING * QW // 2
        arena = sb("arena", [P, ARENA], F32)
        x_ring = arena[:, 0:XRING * XT].rearrange("p (r t b k n) -> p r t b k n", r=XRING, t=T, b=PAIR, k=KC)
        lif1_state = arena[:, XRING * XT:XRING * XT + KC * PN]
        spikes_turned = arena[:, XRING * XT + KC * PN:ARENA].bitcast(F16).rearrange(
            "p (r i c) -> p r i c", r=STRING, i=2)
        w1_again = arena[:, 0:HC * C].rearrange("p (m c) -> p m c", m=HC)
        CW = C + 1
        o = XT
        cov = arena[:, o:o + KC * CW].rearrange("p (k c) -> p k c", k=KC)
        o += KC * CW + 1
        cov_hi = arena[:, o:o + KC * 193].bitcast(F16).rearrange("p (k c) -> p k c", k=KC)[:, :, 0:CW]
        o += KC * 193
        cov_lo = arena[:, o:o + KC * 193].bitcast(F16).rearrange("p (k c) -> p k c", k=KC)[:, :, 0:CW]
        o += KC * 193
        diag = arena[:, o:o + C].rearrange("p (k c) -> p k c", k=KC)
        o += C
        rate_row = arena[:, o:o + C]
        o += C
        outer = arena[:, o:o + C]
        assert o + C <= 2 * XT
        prod = arena[:, 2 * XT:2 * XT + 2 * C].rearrange("p (r c) -> p r c", r=2)
        hid = arena[:, 0:4 * TN].rearrange("p (r m n) -> p r m n", r=2, m=2)
        o = 4 * TN
        spikes2 = arena[:, o:o + 2 * HC * TN // 4].bitcast(F8).rearrange("p (r m n) -> p r m n", r=2, m=HC)
        o += 2 * HC * TN // 4
        resid = arena[:, o:o + KC * TN].rearrange("p (u k n) -> p u k n", u=T * PAIR, k=KC)
        o += KC * TN
        lif2_state = arena[:, o:o + 2 * PN].rearrange("p (m n) -> p m n", m=2)
        assert o + 2 * PN <= ARENA

        psum = ctx.enter_context(nc.psum_tensor("psum", [P, 8, 512], F32))
        halves = psum[:, :, :].rearrange("p (f t) (b n) -> p f (t b) n", f=2, b=PAIR)[:, :, :, 0:N]
        gram = [psum[:, 0, 0:C], psum[:, 1, 0:C - P], psum[:, 2, 0:C - 2 * P]]
        GN_BANK, RATE_BANK, KEPT_BANK = 7, 3, 3

        w_loaded = [sem("w1_loaded"), sem("w2_loaded")]
        par_loaded = sem("par_loaded")
        consts_set = sem("consts_set")
        w_scales = sem("w_scales")
        w_scaled = sem("w_scaled")
        w_transposed = sem("w_transposed")
        w_hi_set = sem("w_hi_set")
        w_lo_set = sem("w_lo_set")
        x_loaded = [[sem(f"x_loaded{r}_{t}") for t in range(T)] for r in range(XRING)]
        x_free = sem("x_free")
        dve_step = sem("dve_step")
        gn_sums = sem("gn_sums")
        gn_squared = sem("gn_squared")
        root_in = sem("root_in")
        root_out = sem("root_out")
        affine_part = sem("affine_part")
        affine1_ready = sem("affine1_ready")
        affine1_copied = sem("affine1_copied")
        y_act = sem("y_act")
        y_pool = sem("y_pool")
        lif1_step = sem("lif1_step")
        spikes1_ready = sem("spikes1_ready")
        spikes1_part = sem("spikes1_part")
        spikes1_kept = [sem(f"spikes1_kept{r}") for r in range(2)]
        turned = sem("turned")
        turned_ready = sem("turned_ready")
        gram_step = sem("gram_step")
        zeros_set = sem("zeros_set")
        kept_weights = sem("kept_weights")
        kept_done = sem("kept_done")
        kept_read = sem("kept_read")
        kept_stored = [sem(f"kept_stored{r}") for r in range(2)]
        kept_loaded = [sem(f"kept_loaded{r}") for r in range(4)]
        kept_hidden = sem("kept_hidden")
        last_ready = sem("last_ready")
        diag_ready = sem("diag_ready")
        rates_ready = sem("rates_ready")
        cov_ready = sem("cov_ready")
        wcov_ready = sem("wcov_ready")
        wcov_read = sem("wcov_read")
        affine2_ready = sem("affine2_ready")
        spikes1_back = sem("spikes1_back")
        g1_done = sem("g1_done")
        g1_read = sem("g1_read")
        lif2_step = sem("lif2_step")
        spikes2_ready = sem("spikes2_ready")
        g2_done = sem("g2_done")
        g2_read = sem("g2_read")
        final_done = sem("final_done")
        final_read = sem("final_read")
        resid_loaded = sem("resid_loaded")
        resid_biased = sem("resid_biased")
        stored = sem("stored")
        waited = {e: sem(f"waited_{e}") for e in ("sp", "act", "dve", "pool", "pe")}

        def wait_first(eng, name, semaphore, value):
            eng.wait_ge(semaphore, value)
            if not isinstance(value, int):
                eng.sem_inc(waited[name], 1)

        def dram(a, t, g):
            return a[t, bass.ds(g * PAIR, PAIR), :, :].rearrange("b (p k) n -> p b (k n)", k=KC)

        def pair_of(n):
            return (n + G - XRING) % G if isinstance(n, int) else n - XRING

        def second_pass(eng, tile):
            for r in range(XRING):
                tile(r, r, r >= FIRST_KEPT)
            with eng.Fori(1, G // XRING - 1) as i:
                for r in range(XRING):
                    tile(i * XRING + r, r, True)
            for r in range(XRING):
                tile(G - XRING + r, r, G - XRING + r < FIRST_KEPT + HC)

        block = ctx.enter_context(nc.Block())

        @block.sync
        def _(sp):
            def load_tile(g, r):
                for t in range(T):
                    sp.dma_start(x_ring[:, r, t, :, :, :].rearrange("p b k n -> p b (k n)"), dram(x, t, g)
                                 ).then_inc(x_loaded[r][t], 16)

            with sp.Fori(0, G // XRING) as i:
                for r in range(XRING):
                    wait_first(sp, "sp", x_free, i * XRING + (r + 1))
                    load_tile(i * XRING + r, r)
            def second_pass_moves(g, r, kept):
                if isinstance(g, int) and g == G - 2:
                    for n in range(2):
                        sp.wait_ge(kept_stored[n], 16 * HC)
                wait_first(sp, "sp", spikes1_ready, g + 1)
                if isinstance(g, int) and g >= G - BY_TIME:
                    sp.wait_ge(spikes1_part, (g - (G - BY_TIME) + 1) * (T - 1))
                sp.dma_start(spikes1_all[:, bass.ds(g * SPIKE_WORDS, SPIKE_WORDS)],
                             spikes1[:, r % 2, :, :].rearrange("p k n -> p (k n)").bitcast(U32)
                             ).then_inc(spikes1_kept[r % 2], 16)
                if not (isinstance(g, int) and g >= G - XRING):
                    load_tile(pair_of(g + XRING), r)
                elif g == G - XRING:
                    sp.dma_start(w1_again, fc1_w.rearrange("(m p) c -> p m c", p=P)).then_inc(w_loaded[0], 16)
                if kept:
                    m = g - FIRST_KEPT
                    for n in range(2):
                        part = slice(2 * n * PN, (2 * n + 2) * PN)
                        wait_first(sp, "sp", kept_read, m * T + (2 * n + 2))
                        sp.dma_start(h_kept[bass.ds(m, 1), :, part].rearrange("o p n -> (o p) n"), h_stage[:, part]
                                     ).then_inc(kept_stored[n], 16)

            second_pass(sp, second_pass_moves)

            def load_resid(n):
                for t in range(T):
                    sp.dma_start(resid[:, t * PAIR:(t + 1) * PAIR, :, :].rearrange("p b k n -> p b (k n)"),
                                 dram(x, t, pair_of(n))).then_inc(resid_loaded, 16)

            sp.wait_ge(affine2_ready, 1)
            def store_results(n):
                wait_first(sp, "sp", g2_read, n * G2_JOBS + (G2_JOBS + 1))
                for t in range(T):
                    sp.dma_start(dram(out, t, pair_of(n + 1)),
                                 resid[:, t * PAIR:(t + 1) * PAIR, :, :].rearrange("p b k n -> p b (k n)")
                                 ).then_inc(stored, 16)
                wait_first(sp, "sp", stored, n * (16 * T) + 16 * T)

            load_resid(1)
            for n in range(XRING - 1):
                store_results(n)
                load_resid(n + 2)
            with sp.Fori(XRING - 1, G - 2) as n:
                store_results(n)
                load_resid(n + 2)
            store_results(G - 2)
            load_resid(0)
            for k in range(KC):
                if k < KC - 1:
                    sp.wait_ge(g2_read, (G - 1) * G2_JOBS + k + 2)
                for t in range(T):
                    if k == KC - 1:
                        sp.wait_ge(final_read, t + 1)
                    first = pair_of(0) * PAIR
                    sp.dma_start(out[t, first:first + PAIR, :, :].rearrange("b (p k) n -> p b k n", k=KC)[:, :, k, :],
                                 resid[:, t * PAIR:(t + 1) * PAIR, k, :]).then_inc(stored, 16)
            sp.wait_ge(stored, 16 * T * (G - 1 + KC))

        @block.scalar
        def _(act):
            act.dma_start(w1_nat, fc1_w.rearrange("(m p) c -> p m c", p=P)).then_inc(w_loaded[0], 16)
            act.dma_start(w2_nat, fc2_w.rearrange("(p k) h -> p k h", k=KC)).then_inc(w_loaded[1], 16)
            for i, v in enumerate((fc2_b, fc2_gamma, fc2_beta)):
                act.dma_start(par2[:, i, :], v.rearrange("(p k) -> p k", k=KC)).then_inc(par_loaded, 16)
            for i, v in enumerate((fc1_b, fc1_gamma, fc1_beta)):
                act.dma_start(par1[:, i, :], v.rearrange("(m p) -> p m", p=P)).then_inc(par_loaded, 16)
            act.wait_ge(w_scales, 1)
            for m in range(HC):
                act.activation(w1_nat[:, m, :], w1_nat[:, m, :], ACT.Copy, scale=scale1[:, 0, m:m + 1]
                               ).then_inc(w_scaled, 1)
            act.wait_ge(w_scales, 2)
            for k in range(KC):
                act.activation(w2_nat[:, k, :], w2_nat[:, k, :], ACT.Copy, scale=scale2[:, 0, k:k + 1]
                               ).then_inc(w_scaled, 1)
            for q in range(9 + HC):
                act.wait_ge(w_transposed, q + 1)
                if q >= 4:
                    act.wait_ge(w_lo_set, q - 3)
                if q < 9:
                    cols, high = 512, w1_hi[:, q // 3, (q % 3) * 512:(q % 3 + 1) * 512]
                else:
                    cols, high = C, w2_hi[:, q - 9, :]
                act.activation(w_turned[:, q % 4, 0:cols], psum[:, q % 4, 0:cols], ACT.Copy).then_inc(w_hi_set, 1)
                act.activation(high, psum[:, q % 4, 0:cols], ACT.Copy).then_inc(w_hi_set, 1)
            for n in range(2):
                act.wait_ge(root_in, n + 1)
                src, dst = ((gn_var, gn_rstd), (tiny[:, 2, 0:KC], tiny[:, 3, 0:KC]))[n]
                act.activation(dst, src, ACT.Sqrt).then_inc(root_out, 1)

            act.sem_inc(y_act, XRING * T)
            act.sem_inc(turned_ready, 2)

            def normalise(g, r, rounds, t):
                if t == 0:
                    act.wait_ge(affine1_copied, g + 1)
                act.wait_ge(x_loaded[r][t], rounds)
                act.activation(x_ring[:, r, t, :, 0, :], x_ring[:, r, t, :, 0, :], ACT.Identity,
                               scale=affine1_now[:, r, t * KC:t * KC + 1],
                               bias=affine1_now[:, r, T * KC + t * KC:T * KC + t * KC + 1]).then_inc(y_act, 1)

            def turn_out(g, r, q):
                place = (r * NQ + q)
                act.wait_ge(turned, g * NQ + (q + 1 + 2 * NQ))
                act.wait_ge(gram_step, g * NQ + (q + 1))
                s = 4 + 2 * (place % 2)
                act.activation(spikes_turned[0:TOK, place % STRING, :, :], psum[0:TOK, s:s + 2, 0:C], ACT.Copy
                               ).then_inc(turned_ready, 1)

            def keep_out(g, t):
                m = g - FIRST_KEPT
                act.wait_ge(kept_done, m * T + (t + 1))
                if not (isinstance(m, int) and m == 0):
                    act.wait_ge(kept_stored[t // 2], m * 16)
                act.activation(h_stage[:, t * PN:(t + 1) * PN], psum[:, KEPT_BANK, 0:PN], ACT.Copy).then_inc(kept_read, 1)

            X_ROUND = 16
            first = (G // XRING) * X_ROUND
            for g in range(AHEAD):
                for t in range(T):
                    normalise(g, g, first, t)

            def second_pass_act(g, r, kept):
                more = not (isinstance(g, int) and g >= G - AHEAD)
                rounds = (g - r) * (X_ROUND // XRING) + (first + (X_ROUND if r + AHEAD >= XRING else 0))
                for q in range(NQ):
                    turn_out(g, r, q)
                    if kept and q in KEPT_AFTER:
                        keep_out(g, KEPT_AFTER.index(q))
                    if more and q % 2 == 0:
                        normalise(g + AHEAD, (r + AHEAD) % XRING, rounds, q // 2)

            second_pass(act, second_pass_act)

            act.wait_ge(root_in, 3)
            act.activation(tiny[:, 3, :], tiny[:, 2, :], ACT.Sqrt).then_inc(root_out, 1)

            def hidden(s, m):
                wait_first(act, "act", g1_done, s * G1_JOBS + (m + 1))
                if isinstance(s, int) and s * HP + m // 2 < 2:
                    pass
                else:
                    wait_first(act, "act", spikes2_ready, s * HP + (m // 2 - 1))
                act.activation(hid[:, (m // 2) % 2, m % 2, :].rearrange("p (u n) -> p u n", n=N),
                               halves[:, job_half(s, m), :, :], ACT.Identity,
                               scale=affine2[:, 0, m:m + 1], bias=affine2[:, 1, m:m + 1]).then_inc(g1_read, 1)

            def job_half(s, m):
                if isinstance(s, int) and s == 0:
                    return m % 2
                return (m + m // 4 + parity[0]) % 2

            parity = [0]
            act.wait_ge(affine2_ready, 1)
            for m in range(HC):
                hidden(0, m)
            with act.Fori(0, (G - 4) // 2) as i:
                for u in range(2):
                    parity[0] = u
                    for m in range(HC):
                        hidden(i * 2 + (u + 1), m)
            parity[0] = 0
            for m in range(HC):
                hidden(G - 3, m)
            def load_kept(q):
                if q >= KEPT_RING:
                    act.wait_ge(last_ready, q - KEPT_RING + 1)
                act.dma_start(hid_last[:, q % KEPT_RING, :, :], h_kept[2 * q:2 * q + 2, :, :].rearrange("m p n -> p m n")
                              ).then_inc(kept_loaded[q % KEPT_RING], 16)

            def hidden_kept(q):
                act.wait_ge(kept_loaded[q % KEPT_RING], 16 * (q // KEPT_RING + 1))
                v = hid_last[:, q % KEPT_RING, :, :]
                for i in range(2):
                    m = 2 * q + i
                    act.activation(v[:, i, :], v[:, i, :], ACT.Identity,
                                   scale=affine2[:, 0, m:m + 1], bias=affine2[:, 1, m:m + 1]).then_inc(kept_hidden, 1)

            for n in range(2):
                act.wait_ge(kept_stored[n], 16 * HC)
            act.wait_ge(spikes1_back, G - 1)
            for q in range(KEPT_RING):
                load_kept(q)
            parity[0] = (G - 3) % 2
            for k in range(KC):
                for m in range(4 * k, 4 * k + 4):
                    hidden(G - 2, m)
                hidden_kept(k)
            hidden_kept(KC)
            for q in range(KEPT_RING, HP):
                load_kept(q)
                hidden_kept(q)

        @block.vector
        def _(dve):
            count = [0]

            def link(ins):
                count[0] += 1
                ins.then_inc(dve_step, 1)
                dve.wait_ge(dve_step, count[0])

            dve.sem_inc(x_free, XRING)
            for n, (w, sc, rows) in enumerate(((w1_nat, scale1, HC), (w2_nat, scale2, KC))):
                dve.wait_ge(w_loaded[n], 16)
                big = tiny[:, 0, 0:rows]
                least = tiny[:, 1, 0:rows]
                link(dve.tensor_reduce(big, w, AX.X, ALU.max))
                link(dve.tensor_reduce(least, w, AX.X, ALU.min))
                link(dve.scalar_tensor_tensor(out=big, in0=least, scalar=-1.0, in1=big, op0=ALU.mult, op1=ALU.max))
                link(dve.tensor_scalar(big, big, 2.0 ** -100, None, ALU.max))
                expo = tiny[:, 1, 0:rows].bitcast(I32)
                link(dve.tensor_scalar(expo, big.bitcast(I32), 0x7F800000, None, ALU.bitwise_and))
                link(dve.tensor_scalar(sc[:, 0, :].bitcast(I32), expo, -1.0, float(268 << 23), ALU.mult, ALU.add))
                link(dve.tensor_scalar(sc[:, 1, :].bitcast(I32), expo, float(-(14 << 23)), None, ALU.add))
                dve.sem_inc(w_scales, 1)

            with dve.Fori(0, G // XRING) as i:
                for r in range(XRING):
                    for t in range(T):
                        wait_first(dve, "dve", x_loaded[r][t], i * 16 + 16)
                        for k in range(KC):
                            e = t * KC + k
                            ins = dve.bn_stats(stats[:, bass.ds((i * XRING + r) * (6 * T * KC) + 6 * e, 6)],
                                               x_ring[:, r, t, :, k, :])
                    ins.then_inc(x_free, 1)
            dve.wait_ge(x_free, G + XRING)

            st = stats.rearrange("p (s v) -> p v s", v=6)
            link(dve.tensor_tensor(mu, st[:, 1, :], st[:, 4, :], ALU.add))
            link(dve.tensor_scalar(mu, mu, 0.5, None, ALU.mult))
            dve.sem_inc(gn_sums, 1)
            link(dve.tensor_tensor(tmp_a, st[:, 1, :], st[:, 4, :], ALU.subtract))
            link(dve.tensor_tensor(tmp_a, tmp_a, tmp_a, ALU.mult))
            link(dve.tensor_tensor(m2, st[:, 2, :], st[:, 5, :], ALU.add))
            link(dve.scalar_tensor_tensor(out=m2, in0=tmp_a, scalar=PN / 4.0, in1=m2, op0=ALU.mult, op1=ALU.add))
            link(dve.tensor_scalar(m2, m2, 1.0 / PN, None, ALU.mult))

            def by_chunk(v):
                return v.rearrange("p (s k) -> p s k", k=KC)

            def over_chunks(v):
                return v.unsqueeze(2).to_broadcast([P, G * T, KC])

            def over_slots(v):
                return v.unsqueeze(1).to_broadcast([P, G * T, KC])

            def newton_rsqrt(dst, var, tmp, n):
                dve.sem_inc(root_in, 1)
                dve.wait_ge(root_out, n)
                link(dve.reciprocal(dst, dst))
                link(dve.tensor_tensor(tmp, dst, dst, ALU.mult))
                link(dve.tensor_tensor(tmp, tmp, var, ALU.mult))
                link(dve.tensor_scalar(tmp, tmp, -0.5, 1.5, ALU.mult, ALU.add))
                link(dve.tensor_tensor(dst, dst, tmp, ALU.mult))

            sums = psum[:, GN_BANK, 0:G * T]
            dve.wait_ge(gn_sums, 2)
            link(dve.tensor_scalar(gn_mean, sums, 1.0 / C, None, ALU.mult))
            link(dve.tensor_tensor(by_chunk(mu), by_chunk(mu), over_chunks(gn_mean), ALU.subtract))
            link(dve.tensor_tensor(tmp_a, mu, mu, ALU.mult))
            link(dve.tensor_tensor(tmp_a, tmp_a, m2, ALU.add))
            dve.sem_inc(gn_sums, 1)
            dve.wait_ge(gn_sums, 4)
            link(dve.tensor_scalar(gn_var, sums, 1.0 / C, EPS, ALU.mult, ALU.add))
            newton_rsqrt(gn_rstd, gn_var, gn_tmp, 1)
            link(dve.tensor_tensor(by_chunk(mu), by_chunk(mu), over_chunks(gn_rstd), ALU.mult))
            bn_mean, bn_var, bn_rstd, bn_tmp, bn_scale = (tiny[:, i, 0:KC] for i in (1, 2, 3, 4, 5))
            link(dve.tensor_reduce(bn_mean, mu.rearrange("p (s k) -> p k s", k=KC), AX.X, ALU.add))
            link(dve.tensor_scalar(bn_mean, bn_mean, 1.0 / (G * T), None, ALU.mult))
            dve.tensor_tensor(gn_tmp, gn_rstd, gn_rstd, ALU.mult).then_inc(gn_squared, 1)
            link(dve.tensor_tensor(by_chunk(tmp_a), by_chunk(mu), over_slots(bn_mean), ALU.subtract))
            dve.wait_ge(gn_squared, 1)
            link(dve.tensor_tensor(by_chunk(tmp_b), by_chunk(m2), over_chunks(gn_tmp), ALU.mult))
            link(dve.tensor_tensor(tmp_a, tmp_a, tmp_a, ALU.mult))
            link(dve.tensor_tensor(tmp_a, tmp_a, tmp_b, ALU.add))
            link(dve.tensor_reduce(bn_var, tmp_a.rearrange("p (s k) -> p k s", k=KC), AX.X, ALU.add))
            link(dve.tensor_scalar(bn_var, bn_var, 1.0 / (G * T), EPS, ALU.mult, ALU.add))
            newton_rsqrt(bn_rstd, bn_var, bn_tmp, 2)
            dve.wait_ge(par_loaded, 96)
            dve.scalar_tensor_tensor(out=gn_shift, in0=gn_mean, scalar=-1.0, in1=gn_rstd,
                                     op0=ALU.mult, op1=ALU.mult).then_inc(affine_part, 1)
            dve.tensor_tensor(bn_scale, par2[:, 1, :], bn_rstd, ALU.mult).then_inc(affine_part, 1)
            dve.wait_ge(affine_part, 2)
            biases = [affine1[:, :, T * KC + k:2 * T * KC:KC] for k in range(KC)]
            for k, b in enumerate(biases):
                dve.tensor_scalar(b, gn_shift.rearrange("p (g t) -> p g t", g=G), bn_mean[:, k:k + 1],
                                  bn_scale[:, k:k + 1], ALU.subtract, ALU.mult).then_inc(affine_part, 1)
            for k in range(KC):
                dve.tensor_scalar(affine1[:, :, k:T * KC:KC], gn_rstd.rearrange("p (g t) -> p g t", g=G),
                                  bn_scale[:, k:k + 1], 1.0 / TAU, ALU.mult, ALU.mult).then_inc(affine_part, 1)
            dve.wait_ge(affine_part, 2 + KC)
            for k, b in enumerate(biases):
                dve.tensor_scalar(b, b, par2[:, 2, k:k + 1], 1.0 / TAU, ALU.add, ALU.mult).then_inc(affine_part, 1)
            dve.wait_ge(affine_part, 2 + 3 * KC)
            dve.sem_inc(affine1_ready, 1)

            KEEP = 1.0 - 1.0 / TAU

            HALF = KC * N

            def lif1(g, r, by_time=False):
                flat = [[x_ring[:, r, t, b, :, :].rearrange("p k n -> p (k n)") for b in range(PAIR)] for t in range(T)]
                state = [lif1_state[:, b * HALF:(b + 1) * HALF] for b in range(PAIR)]
                per_tile = 2 * PAIR * (T - 1)
                n = 0

                def ring_free():
                    dve.wait_ge(turned, (g + 1) * NQ)
                    dve.wait_ge(spikes1_kept[r % 2], kept_round(g, r))

                def spikes(t0, t1, done):
                    wait_first(dve, "dve", lif1_step, g * per_tile + done)
                    return dve.tensor_scalar(
                        spikes1[:, r % 2, :, t0 * PN:t1 * PN].rearrange("p k (u n) -> p u k n", n=N),
                        x_ring[:, r, t0:t1, :, :, :].rearrange("p t b k n -> p (t b) k n"),
                        1.0, None, ALU.is_ge, saturate=False)

                for t in range(T - 1):
                    if t == 0:
                        dve.wait_ge(y_act, g * T + (1 + XRING * T))
                        dve.wait_ge(y_pool, g * T + 1)
                    for b in range(PAIR):
                        if t > 0:
                            dve.wait_ge(lif1_step, g * per_tile + (n - 1))
                        dve.scalar_tensor_tensor(out=state[b], in0=flat[t][b], scalar=1.0, in1=flat[t][b],
                                                 op0=ALU.is_lt, op1=ALU.mult).then_inc(lif1_step, 1)
                        n += 1
                    if by_time:
                        if t == 0:
                            ring_free()
                        spikes(t, t + 1, n - PAIR).then_inc(spikes1_part, 1)
                    dve.wait_ge(y_act, g * T + (t + 2 + XRING * T))
                    dve.wait_ge(y_pool, g * T + (t + 2))
                    for b in range(PAIR):
                        dve.wait_ge(lif1_step, g * per_tile + (n - 1))
                        dve.scalar_tensor_tensor(out=flat[t + 1][b], in0=state[b], scalar=KEEP, in1=flat[t + 1][b],
                                                 op0=ALU.mult, op1=ALU.add).then_inc(lif1_step, 1)
                        n += 1
                if not by_time:
                    ring_free()
                spikes(T - 1 if by_time else 0, T, n).then_inc(spikes1_ready, 1)

            def kept_round(g, r):
                return g * 8 - 8 * (r % 2) + 16

            dve.sem_inc(g2_read, 1)
            dve.sem_inc(spikes1_kept[0], 16)
            dve.sem_inc(spikes1_kept[1], 16)
            with dve.Fori(0, G // XRING - 1) as i:
                for r in range(XRING):
                    lif1(i * XRING + r, r)
            for g in range(G - XRING, G):
                lif1(g, g % XRING, g >= G - BY_TIME)

            dve.wait_ge(gram_step, G * NQ + STRING)
            rate = tiny[:, 6, 0:KC]
            for k in range(KC):
                dve.tensor_tensor(diag[:, k, :], gram[k][:, 0:P], ident[:, :], ALU.mult).then_inc(diag_ready, 1)
            dve.wait_ge(diag_ready, KC)
            link(dve.tensor_reduce(rate, diag, AX.X, ALU.add))
            link(dve.tensor_scalar(rate, rate, 1.0 / TOKENS, None, ALU.mult))
            dve.wait_ge(rates_ready, 1)
            link(dve.tensor_scalar(rate_row, psum[:, RATE_BANK, 0:C], COVSCALE / TOKENS, None, ALU.mult))
            for k in range(KC):
                link(dve.tensor_scalar(outer[:, k * P:C], rate_row[:, k * P:C], rate[:, k:k + 1], None, ALU.mult))
                if k < KC - 1:
                    dve.tensor_scalar(cov[:, k, C:CW], rate[:, k:k + 1], COVSCALE, None, ALU.mult)
                    link(dve.scalar_tensor_tensor(out=cov[:, k, k * P:C], in0=gram[k], scalar=COVSCALE / TOKENS,
                                                  in1=outer[:, k * P:C], op0=ALU.mult, op1=ALU.subtract))
                    link(dve.tensor_scalar(cov[:, k, (k + 1) * P:C], cov[:, k, (k + 1) * P:C], 2.0, None, ALU.mult))
                else:
                    dve.tensor_scalar(cov[:, k, C:CW], rate[:, k:k + 1], COVSCALE, None, ALU.mult)
                    link(dve.scalar_tensor_tensor(out=cov[:, k, k * P:C], in0=gram[k], scalar=COVSCALE / TOKENS,
                                                  in1=outer[:, k * P:C], op0=ALU.mult, op1=ALU.subtract))
                link(dve.tensor_copy(cov_hi[:, k, k * P:CW], cov[:, k, k * P:CW]))
                dve.tensor_tensor(cov_lo[:, k, k * P:CW], cov[:, k, k * P:CW], cov_hi[:, k, k * P:CW], ALU.subtract
                                  ).then_inc(cov_ready, 1)
            h_var, h_mean = tiny[:, 7, :], tiny[:, 8, :]
            dve.wait_ge(w_loaded[0], 32)
            for m in range(HC):
                dve.wait_ge(wcov_ready, m + 1)
                bank = 4 + m % 4
                if m >= 2:
                    dve.wait_ge(wcov_read, 2 * m - 2)
                dve.tensor_copy(h_mean[:, m:m + 1], psum[:, bank, C:CW]).then_inc(wcov_read, 1)
                dve.tensor_tensor_reduce(prod[:, m % 2, :].rearrange("p (k c) -> p k c", k=KC),
                                         psum[:, bank, 0:C].rearrange("p (k c) -> p k c", k=KC),
                                         w1_again[:, m, :].rearrange("p (c k) -> p k c", k=KC), 1.0, 0.0,
                                         ALU.mult, ALU.add, h_var[:, m:m + 1]).then_inc(wcov_read, 1)
            dve.wait_ge(wcov_read, 2 * HC)
            bias, gamma, beta = par1[:, 0, :], par1[:, 1, :], par1[:, 2, :]
            inv = scale1[:, 1, :]
            t2, t3, t4 = tiny[:, 2, :], tiny[:, 3, :], tiny[:, 4, :]
            for v in (h_var, h_mean):
                link(dve.tensor_tensor(v, v, inv, ALU.mult))
                link(dve.tensor_scalar(v, v, 1.0 / COVSCALE, None, ALU.mult))
            link(dve.tensor_tensor(h_mean, h_mean, bias, ALU.add))
            link(dve.tensor_scalar(t2, h_var, EPS, None, ALU.add))
            newton_rsqrt(t3, t2, t4, 3)
            link(dve.tensor_tensor(t3, t3, gamma, ALU.mult))
            link(dve.scalar_tensor_tensor(out=affine2[:, 0, :], in0=inv, scalar=1.0 / TAU, in1=t3,
                                          op0=ALU.mult, op1=ALU.mult))
            link(dve.tensor_tensor(t4, bias, h_mean, ALU.subtract))
            link(dve.tensor_tensor(t4, t4, t3, ALU.mult))
            link(dve.tensor_tensor(t4, t4, beta, ALU.add))
            link(dve.tensor_scalar(affine2[:, 1, :], t4, 1.0 / TAU, None, ALU.mult))
            dve.sem_inc(affine2_ready, 1)

            def lif2(pairs, v):
                n = 0
                for t in range(T - 1):
                    dve.scalar_tensor_tensor(out=lif2_state, in0=v[t], scalar=1.0, in1=v[t],
                                             op0=ALU.is_lt, op1=ALU.mult).then_inc(lif2_step, 1)
                    n += 1
                    dve.wait_ge(lif2_step, pairs * 6 + n)
                    dve.scalar_tensor_tensor(out=v[t + 1], in0=lif2_state, scalar=KEEP, in1=v[t + 1],
                                             op0=ALU.mult, op1=ALU.add).then_inc(lif2_step, 1)
                    n += 1
                    if t < T - 2:
                        dve.wait_ge(lif2_step, pairs * 6 + n)

            def by_time(v):
                return [v[:, :, t * PN:(t + 1) * PN] for t in range(T)]

            def lif2_pair(s, q, slot, kept=0):
                pairs = s * HP + (q + kept)
                v = hid[:, q % 2, :, :]
                dve.wait_ge(g1_read, s * G1_JOBS + 2 * (q + 1))
                lif2(pairs, by_time(v))
                if q == 0 and not (isinstance(s, int) and s < 2):
                    dve.wait_ge(g2_done, (s - 1) * G2_JOBS + 1)
                wait_first(dve, "dve", lif2_step, pairs * 6 + 6)
                dve.tensor_scalar(spikes2[:, slot, 2 * q:2 * q + 2, :], v, 1.0, None, ALU.is_ge, saturate=False
                                  ).then_inc(spikes2_ready, 1)

            def lif2_kept(q, pairs):
                v = hid_last[:, q % KEPT_RING, :, :]
                dve.wait_ge(kept_hidden, 2 * (q + 1))
                lif2(pairs, by_time(v))
                wait_first(dve, "dve", lif2_step, pairs * 6 + 6)
                dve.tensor_scalar(spikes2_last[:, 2 * q:2 * q + 2, :], v, 1.0, None, ALU.is_ge, saturate=False
                                  ).then_inc(last_ready, 1)

            def result(n, k, half):
                dve.wait_ge(g2_done, n * G2_JOBS + (k + 2))
                dve.wait_ge(resid_biased, n * G2_JOBS + (k + 1))
                dve.scalar_tensor_tensor(out=resid[:, :, k, :], in0=halves[:, half, :, :], scalar=scale2[:, 1, k:k + 1],
                                         in1=resid[:, :, k, :], op0=ALU.mult, op1=ALU.add).then_inc(g2_read, 1)

            def step(s, slot, first_result, kept):
                for k in range(KC):
                    for q in (2 * k, 2 * k + 1):
                        lif2_pair(s, q, slot, k if kept else 0)
                    result(s - 1, k, (first_result + k) % 2)
                    if kept:
                        lif2_kept(k, s * HP + 3 * k + 2)

            for q in range(HP):
                lif2_pair(0, q, 0)
            with dve.Fori(0, (G - 4) // 2) as i:
                for u in range(2):
                    step(i * 2 + (u + 1), (u + 1) % 2, u, False)
            step(G - 3, 1, 0, False)
            step(G - 2, 0, 1, True)
            for s in (G - 1, G):
                for k in range(KC):
                    if s == G - 1:
                        lif2_kept(KC + k, s * HP + KC + k)
                    half = (s - (G - 1) + k) % 2
                    if s < G or k < KC - 1:
                        result(s - 1, k, half)
                        continue
                    dve.wait_ge(resid_biased, G * G2_JOBS)
                    for t in range(T):
                        at_t = slice(t * PAIR, (t + 1) * PAIR)
                        dve.wait_ge(final_done, t + 1)
                        dve.scalar_tensor_tensor(out=resid[:, at_t, k, :], in0=halves[:, half, at_t, :],
                                                 scalar=scale2[:, 1, k:k + 1], in1=resid[:, at_t, k, :],
                                                 op0=ALU.mult, op1=ALU.add).then_inc(final_read, 1)

        @block.gpsimd
        def _(pool):
            pool.memset(ones[:, :], 1.0).then_inc(consts_set, 1)
            pool.memset(ident[:, :], 0.0).then_inc(consts_set, 1)
            pool.memset(spikes_turned[:, 0, :, :], 0.0).then_inc(zeros_set, 1)
            pool.wait_ge(consts_set, 2)
            pool.affine_select(out=ident[:, :], in_=ident[:, :], compare_op=ALU.not_equal, fill=1.0, base=0,
                               pattern=[[-1, P]], channel_multiplier=1).then_inc(consts_set, 1)
            pool.wait_ge(consts_set, 3)
            pool.tensor_copy(ident8[:, :], ident[:, :], saturate=False).then_inc(consts_set, 1)
            for q in range(9 + HC):
                pool.wait_ge(w_hi_set, 2 * (q + 1))
                if q < 9:
                    cols, at_w = 512, (slice(None), q // 3, slice((q % 3) * 512, (q % 3 + 1) * 512))
                    high, low = w1_hi[at_w], w1_lo[at_w]
                else:
                    cols, high, low = C, w2_hi[:, q - 9, :], w2_lo[:, q - 9, :]
                pool.tensor_tensor(low, w_turned[:, q % 4, 0:cols], high, ALU.subtract).then_inc(w_lo_set, 1)

            pool.wait_ge(affine1_ready, 1)
            X_ROUND = 16
            first = (G // XRING) * X_ROUND

            def copy_affine(g, r):
                wait_first(pool, "pool", y_act, (g + 1) * T)
                if not (isinstance(g, int) and g < XRING):
                    wait_first(pool, "pool", y_pool, (g - (XRING - 1)) * T)
                pool.tensor_copy(affine1_now[:, r:r + 1, :], affine1[:, bass.ds(pair_of(g), 1), :]).then_inc(affine1_copied, 1)

            for g in range(AHEAD):
                copy_affine(g, g)

            def second_pass_pool(g, r, kept):
                if not (isinstance(g, int) and g >= G - AHEAD):
                    copy_affine(g + AHEAD, (r + AHEAD) % XRING)
                wait_first(pool, "pool", affine1_copied, g + 1)
                for t in range(T):
                    wait_first(pool, "pool", x_loaded[r][t], (g - r) * (X_ROUND // XRING) + first)
                    for k in (1, 2):
                        e = t * KC + k
                        ins = pool.tensor_scalar(x_ring[:, r, t, :, k, :], x_ring[:, r, t, :, k, :],
                                                 affine1_now[:, r, e:e + 1],
                                                 affine1_now[:, r, T * KC + e:T * KC + e + 1], ALU.mult, ALU.add)
                    ins.then_inc(y_pool, 1)
                if kept:
                    m = g - FIRST_KEPT
                    if not (isinstance(m, int) and m < 2):
                        wait_first(pool, "pool", kept_done, (m - 1) * T)
                    for w, half in enumerate((w1_hi, w1_lo)):
                        pool.tensor_copy(w_stage[:, r % 2, w, :, :], half[:, :, bass.ds(m * P, P)]
                                         ).then_inc(kept_weights, 1)

            second_pass(pool, second_pass_pool)

            def bring_back(s, slot):
                pool.tensor_copy(spikes1[:, slot, :, :].rearrange("p k n -> p (k n)").bitcast(U32),
                                 spikes1_all[:, bass.ds((s + 1) * SPIKE_WORDS, SPIKE_WORDS)]
                                 ).then_inc(spikes1_back, 1)

            def add_bias(n, k):
                wait_first(pool, "pool", resid_loaded, n * (16 * T) + 16 * T)
                pool.tensor_scalar(resid[:, :, k, :], resid[:, :, k, :], 1.0, par2[:, 0, k:k + 1], ALU.mult, ALU.add
                                   ).then_inc(resid_biased, 1)

            for r in range(2):
                pool.wait_ge(spikes1_kept[r], 16 * (G // 2 + 1))
            pool.wait_ge(turned, (G + 2) * NQ)
            bring_back(0, 0)
            bring_back(1, 1)

            def step(s, slot, more):
                for k in range(KC):
                    add_bias(s - 1, k)
                if more:
                    wait_first(pool, "pool", g1_done, s * G1_JOBS)
                    bring_back(s + 1, slot)

            with pool.Fori(0, (G - 4) // 2) as i:
                for u in range(2):
                    step(i * 2 + (u + 1), u, True)
            step(G - 3, 0, True)
            for s in (G - 2, G - 1, G):
                step(s, 0, False)

        @block.tensor
        def _(pe):
            pe.wait_ge(consts_set, 4)
            for q in range(9 + HC):
                if q >= 4:
                    pe.wait_ge(w_hi_set, 2 * (q - 3))
                if q < 9:
                    pe.wait_ge(w_scaled, 4 * (q % 3 + 1))
                    for i in range(4):
                        ins = pe.transpose(psum[:, q % 4, i * P:(i + 1) * P],
                                           w1_nat[:, 4 * (q % 3) + i, q // 3:C:KC], ident[:, :])
                else:
                    pe.wait_ge(w_scaled, HC + KC)
                    m = q - 9
                    for k in range(KC):
                        ins = pe.transpose(psum[:, q % 4, k * P:(k + 1) * P], w2_nat[:, k, m * P:(m + 1) * P],
                                           ident[:, :])
                ins.then_inc(w_transposed, 1)
            for n, v in enumerate((mu, tmp_a)):
                pe.wait_ge(gn_sums, 2 * n + 1)
                for k in range(KC):
                    ins = pe.matmul(psum[:, GN_BANK, 0:G * T], ones[:, :], v.rearrange("p (s k) -> p k s", k=KC)[:, k, :],
                                    start=(k == 0), stop=(k == KC - 1))
                ins.then_inc(gn_sums, 1)

            pe.wait_ge(zeros_set, 1)
            pe.wait_ge(w_hi_set, 2 * (9 + HC))
            for k in range(KC):
                ins = pe.matmul(gram[k], spikes_turned[:, 0, 0, 0:P], spikes_turned[:, 0, 1, k * P:C], start=True, stop=True)
            ins.then_inc(gram_step, STRING)
            pe.sem_inc(turned, 2 * NQ)
            pe.sem_inc(g2_done, 1)

            def turn(g, r, q):
                place = r * NQ + q
                wait_first(pe, "pe", turned_ready, g * NQ + (q + 1))
                for i in range(2):
                    for k in range(KC):
                        o = (2 * q + i) * TOK
                        ins = pe.matmul(psum[0:TOK, 4 + 2 * (place % 2) + i, k * P:(k + 1) * P],
                                        spikes1[:, r % 2, k, o:o + TOK], ident8[:, :], start=True, stop=True)
                ins.then_inc(turned, 1)

            def add_gram(g, r, q):
                place = (r * NQ + q) % STRING
                wait_first(pe, "pe", turned_ready, g * NQ + (q + 3))
                for i in range(2):
                    for k in range(KC):
                        ins = pe.matmul(gram[k], spikes_turned[0:TOK, place, i, k * P:(k + 1) * P],
                                        spikes_turned[0:TOK, place, i, k * P:C], start=False, stop=True,
                                        skip_group_check=True)
                ins.then_inc(gram_step, 1)

            def keep_product(g, r, t):
                m = g - FIRST_KEPT
                if t == 0:
                    wait_first(pe, "pe", kept_weights, m * 2 + 2)
                if not (isinstance(m, int) and m == 0 and t == 0):
                    wait_first(pe, "pe", kept_read, m * T + t)
                n = 0
                for w in range(2):
                    for k in range(KC):
                        ins = pe.matmul(psum[:, KEPT_BANK, 0:PN], w_stage[:, r % 2, w, k, :],
                                        spikes_tile0[:, k, t * PN:(t + 1) * PN], start=(n == 0), stop=(n == 2 * KC - 1))
                        n += 1
                ins.then_inc(kept_done, 1)

            def second_pass_pe(g, r, kept):
                by_time = isinstance(g, int) and g >= G - BY_TIME
                if not by_time:
                    wait_first(pe, "pe", spikes1_ready, g + 1)
                if isinstance(g, int) and g == FIRST_KEPT:
                    pe.wait_ge(spikes1_kept[0], 32)
                for q in range(NQ):
                    if by_time:
                        t = (2 * TOK * (q + 1) - 1) // PN
                        if t < T - 1:
                            pe.wait_ge(spikes1_part, (g - (G - BY_TIME)) * (T - 1) + t + 1)
                        else:
                            pe.wait_ge(spikes1_ready, g + 1)
                    turn(g, r, q)
                    if not (isinstance(g, int) and g == 0 and q < 2):
                        add_gram(g, r, q - 2)
                    if kept and q in KEPT_AFTER:
                        keep_product(g, r, KEPT_AFTER.index(q))

            second_pass(pe, second_pass_pe)
            for q in (NQ - 2, NQ - 1):
                add_gram(G - 1, XRING - 1, q)

            pe.wait_ge(diag_ready, KC)
            pe.wait_ge(kept_read, HC * T)
            pe.matmul(psum[:, RATE_BANK, 0:C], ones[:, :], diag.rearrange("p k c -> p (k c)"), start=True, stop=True
                      ).then_inc(rates_ready, 1)
            pe.wait_ge(w_lo_set, 9 + HC)
            pe.wait_ge(turned_ready, G * NQ + 2)
            for m0 in range(0, HC, 4):
                order = [(m, k) for k in range(KC) for m in range(4)] if m0 == 0 else [
                    (m, k) for m in range(m0, m0 + 4) for k in range(KC)]
                for m, k in order:
                    if m0 == 0 and m == 0:
                        pe.wait_ge(cov_ready, k + 1)
                    if m0 > 0 and k == 0:
                        pe.wait_ge(wcov_read, 2 * (m - 3))
                    for w in (w1_hi, w1_lo):
                        for cv in (cov_hi, cov_lo):
                            ins = pe.matmul(psum[:, 4 + m % 4, k * P:CW], w[:, k, m * P:(m + 1) * P], cv[:, k, k * P:CW],
                                            start=(k == 0 and w is w1_hi and cv is cov_hi), stop=(k == KC - 1),
                                            skip_group_check=True)
                    if k == KC - 1:
                        ins.then_inc(wcov_ready, 1)

            def first_product(s, m, half, slot):
                n = 0
                for w in (w1_hi, w1_lo):
                    for k in range(KC):
                        for t in range(T):
                            ins = pe.matmul(halves[:, half, t * PAIR:(t + 1) * PAIR, :], w[:, k, m * P:(m + 1) * P],
                                            spikes1[:, slot, k, t * PN:(t + 1) * PN],
                                            start=(n == 0), stop=(n == 2 * KC - 1))
                        n += 1
                ins.then_inc(g1_done, 1)

            def second_product(k, half, spikes):
                n = 0
                for w in (w2_hi, w2_lo):
                    for m in range(HC):
                        for t in range(T):
                            ins = pe.matmul(halves[:, half, t * PAIR:(t + 1) * PAIR, :], w[:, m, k * P:(k + 1) * P],
                                            spikes[:, m, t * PN:(t + 1) * PN],
                                            start=(n == 0), stop=(n == 2 * HC - 1))
                        n += 1
                ins.then_inc(g2_done, 1)

            pe.wait_ge(spikes1_back, 1)
            for m in range(HC):
                if m == 1:
                    pe.wait_ge(wcov_read, 2 * HC)
                if m >= 2:
                    pe.wait_ge(g1_read, m - 1)
                first_product(0, m, m % 2, 0)

            def step(s, slot, first_half):
                wait_first(pe, "pe", spikes1_back, s + 1)
                j = 0
                for k in range(KC):
                    for i in range(4):
                        m = 4 * k + i
                        if j == 0:
                            wait_first(pe, "pe", g1_read, s * G1_JOBS)
                        elif i == 1 and k > 0:
                            wait_first(pe, "pe", g2_read, (s - 1) * G2_JOBS + (k + 1))
                        elif i == 0:
                            wait_first(pe, "pe", g1_read, s * G1_JOBS + m)
                        elif j == 1:
                            wait_first(pe, "pe", g2_read, (s - 1) * G2_JOBS + 1)
                        else:
                            wait_first(pe, "pe", g1_read, s * G1_JOBS + (m - 1))
                        first_product(s, m, (first_half + j) % 2, slot)
                        j += 1
                    if k == 0:
                        wait_first(pe, "pe", spikes2_ready, s * HP)
                    wait_first(pe, "pe", g1_read, s * G1_JOBS + (4 * k + 3))
                    second_product(k, (first_half + j) % 2, spikes2[:, 1 - slot, :, :])
                    j += 1

            with pe.Fori(0, (G - 2) // 2) as i:
                for u in range(2):
                    step(i * 2 + (u + 1), (u + 1) % 2, u)
            for s in (G - 1, G):
                for k in range(KC):
                    if k == 0:
                        if s < G:
                            pe.wait_ge(spikes2_ready, s * HP)
                        else:
                            pe.wait_ge(last_ready, HP)
                        pe.wait_ge(g1_read, (G - 1) * G1_JOBS)
                    pe.wait_ge(g2_read, (s - 1) * G2_JOBS + k)
                    half = (s - (G - 1) + k) % 2
                    if s < G or k < KC - 1:
                        second_product(k, half, spikes2[:, 0, :, :] if s < G else spikes2_last)
                        continue
                    for t in range(T):
                        for w in (w2_hi, w2_lo):
                            for m in range(HC):
                                ins = pe.matmul(halves[:, half, t * PAIR:(t + 1) * PAIR, :],
                                                w[:, m, k * P:(k + 1) * P], spikes2_last[:, m, t * PN:(t + 1) * PN],
                                                start=(w is w2_hi and m == 0), stop=(w is w2_lo and m == HC - 1))
                        ins.then_inc(final_done, 1)


_INS = ["x", "L0_conv_fc1_w", "L0_conv_fc1_b", "L0_conv_fc1_gamma", "L0_conv_fc1_beta",
        "L0_conv_fc2_w", "L0_conv_fc2_b", "L0_conv_fc2_gamma", "L0_conv_fc2_beta"]


def kernel(**inputs):
    import numpy as np
    import concourse.bacc as bacc
    from concourse.bass_utils import run_bass_kernel_spmd

    nc = bacc.Bacc("TRN2", target_bir_lowering=False, num_devices=1)
    arrays, args = {}, []
    for name in _INS:
        a = np.ascontiguousarray(inputs[name])
        arrays[f"in_{name}"] = a
        args.append(nc.dram_tensor(f"in_{name}", a.shape, mybir.dt.from_np(a.dtype), kind="ExternalInput").ap())
    args.append(nc.dram_tensor("out_0", (T, B, C, N), F32, kind="ExternalOutput").ap())
    spiking_mlp(nc, *args)
    r = run_bass_kernel_spmd(nc, [arrays], core_ids=[0])
    return r.results[0]["out_0"]
```
